# Optimizing a Trainium2 kernel written in Bass

```python
import numpy as np
import jax
import jax.numpy as jnp

def _softmax(x, axis=-1):
    return jax.nn.softmax(x, axis=axis)

def _gelu(x):
    return jax.nn.gelu(x, approximate=True)

def _silu(x):
    return jax.nn.silu(x)

def _sigmoid(x):
    return jax.nn.sigmoid(x)

def _layernorm(x, axis=-1, eps=1e-05):
    m = jnp.mean(x, axis=axis, keepdims=True)
    v = jnp.var(x, axis=axis, keepdims=True)
    return (x - m) / jnp.sqrt(v + eps)

def _scatter_add(tgt, idx, src, axis=0):
    return tgt.at[idx].add(src)

def _segment_sum(src, seg, n):
    return jax.ops.segment_sum(src, seg, n)
kernel_name = 'mk_xattn_ffn_d1_seqx_r4_24dd10'

def setup_inputs(seed: int=0):
    np.random.seed(seed)
    _w = jnp.asarray

    def _rec_inputs():
        import jax
        import jax.numpy as jnp
        _rk = jax.random.key(seed)
        x = 7.22e-05 + 1 * jax.random.normal(jax.random.fold_in(_rk, 1), (4, 512, 512), jnp.float32)
        _lenS = 512 - jax.random.randint(jax.random.fold_in(_rk, 7), (4,), 0, max(1, 512 // 4) + 1, jnp.int32)
        _lenS2 = 512 - jax.random.randint(jax.random.fold_in(_rk, 8), (4,), 0, max(1, 512 // 4) + 1, jnp.int32)
        _ctx_512P = jax.random.normal(jax.random.fold_in(_rk, 11), (4, 16, 128), jnp.float32)
        _ctx_512c = jax.random.dirichlet(jax.random.fold_in(_rk, 511), 0.3 * jnp.ones((16,), jnp.float32), (4, 512))
        _ctx_512t = jnp.einsum('bsk,bkd->bsd', _ctx_512c, _ctx_512P)
        _ctx_512t = _ctx_512t * jax.lax.rsqrt(jnp.mean(jnp.square(_ctx_512t)) + 1e-12) * 0.953939
        ctx_512 = -0.000514642 + 1.00011 * (_ctx_512t + 0.3 * jax.random.normal(jax.random.fold_in(_rk, 611), (4, 512, 128), jnp.float32))
        return (x, ctx_512)
    x, ctx_512 = _rec_inputs()

    def _L0_xattn_setup():
        import jax, jax.numpy as jnp
        import numpy as np
        B, S, E = (2, 512, 512)
        QH, KVH = (32, 8)
        D = E // QH
        G = QH // KVH
        DROPOUT = 1.0
        key = jax.random.key(seed)
        k1, k2, k3 = jax.random.split(key, 3)
        q = jax.random.normal(k1, (B, S, E), dtype=jnp.float32)
        k = jax.random.normal(k2, (B, S, E // G), dtype=jnp.float32)
        v = jax.random.normal(k3, (B, S, E // G), dtype=jnp.float32)
        return {'q': q, 'k': k, 'v': v}
    _L0_xattn_all = _L0_xattn_setup()
    _L0_xattn_in = {k: v for k, v in _L0_xattn_all.items() if k in ()}
    del _L0_xattn_all

    def _L0_ffn_setup():
        import jax, jax.numpy as jnp
        import numpy as np
        B, S, D = (2, 512, 512)
        E, H, TOP_K = (8, 352, 2)
        SH = 352
        ROUTED_SCALE = 2.5
        key = jax.random.key(seed)
        ks = jax.random.split(key, 8)
        std = 0.02
        return {'x': jax.random.normal(ks[0], (B, S, D), jnp.float32), 'gate_w': jax.random.normal(ks[1], (E, D), jnp.float32) * std, 'w1': jax.random.normal(ks[2], (E, D, H), jnp.float32) * std, 'w3': jax.random.normal(ks[3], (E, D, H), jnp.float32) * std, 'w2': jax.random.normal(ks[4], (E, H, D), jnp.float32) * std, 'sw1': jax.random.normal(ks[5], (D, SH), jnp.float32) * std, 'sw3': jax.random.normal(ks[6], (D, SH), jnp.float32) * std, 'sw2': jax.random.normal(ks[7], (SH, D), jnp.float32) * std}
    _L0_ffn_all = _L0_ffn_setup()
    _L0_ffn_in = {k: v for k, v in _L0_ffn_all.items() if k in ('gate_w', 'w1', 'w2', 'w3', 'sw1', 'sw2', 'sw3')}
    del _L0_ffn_all
    return {'x': x, 'ctx_512': ctx_512, 'L0_ffn_gate_w': _L0_ffn_in['gate_w'], 'L0_ffn_w1': _L0_ffn_in['w1'], 'L0_ffn_w2': _L0_ffn_in['w2'], 'L0_ffn_w3': _L0_ffn_in['w3'], 'L0_ffn_sw1': _L0_ffn_in['sw1'], 'L0_ffn_sw2': _L0_ffn_in['sw2'], 'L0_ffn_sw3': _L0_ffn_in['sw3']}

def reference(x, ctx_512, L0_ffn_gate_w, L0_ffn_w1, L0_ffn_w2, L0_ffn_w3, L0_ffn_sw1, L0_ffn_sw2, L0_ffn_sw3):
    import jax
    import jax.numpy as jnp

    def _L0_xattn_ref(q, k, v):
        import jax, jax.numpy as jnp
        import numpy as np
        B, S, E = (2, 512, 512)
        QH, KVH = (32, 8)
        D = E // QH
        G = QH // KVH
        DROPOUT = 1.0
        b, s, _ = q.shape
        qh = q.reshape(b, s, KVH, G, D).transpose(0, 2, 3, 1, 4)
        kh = k.reshape(b, s, KVH, D).transpose(0, 2, 1, 3)
        vh = v.reshape(b, s, KVH, D).transpose(0, 2, 1, 3)
        scale = 1.0 / jnp.sqrt(jnp.float32(D))
        scores = jnp.einsum('bkgsd,bktd->bkgst', qh, kh) * scale
        attn = jax.nn.softmax(scores, axis=-1) / DROPOUT
        out = jnp.einsum('bkgst,bktd->bkgsd', attn, vh)
        return out.transpose(0, 3, 1, 2, 4).reshape(b, s, E)

    def _L0_ffn_ref(x, gate_w, w1, w2, w3, sw1, sw2, sw3):
        import jax, jax.numpy as jnp
        import numpy as np
        B, S, D = (2, 512, 512)
        E, H, TOP_K = (8, 352, 2)
        SH = 352
        ROUTED_SCALE = 2.5
        b, s, d = x.shape
        xt = x.reshape(b * s, d)
        scores = jax.nn.sigmoid(xt @ gate_w.T)
        top_scores, top_idx = jax.lax.top_k(scores, TOP_K)
        top_scores = top_scores / (jnp.sum(top_scores, axis=-1, keepdims=True) + 1e-20)
        top_scores = top_scores * ROUTED_SCALE
        combine = jnp.sum(jax.nn.one_hot(top_idx, E, dtype=xt.dtype) * top_scores[..., None], axis=1)
        h = jnp.einsum('td,edh->eth', xt, w1)
        u = jnp.einsum('td,edh->eth', xt, w3)
        y = jnp.einsum('eth,ehd->etd', jax.nn.silu(h) * u, w2)
        routed = jnp.einsum('etd,te->td', y, combine)
        shared = jax.nn.silu(xt @ sw1) * (xt @ sw3) @ sw2
        return (routed + shared).reshape(b, s, d)
    x = x + _L0_xattn_ref(_layernorm(x, axis=-1), ctx_512, ctx_512)
    x = x + _L0_ffn_ref(_layernorm(x, axis=-1), L0_ffn_gate_w, L0_ffn_w1, L0_ffn_w2, L0_ffn_w3, L0_ffn_sw1, L0_ffn_sw2, L0_ffn_sw3)
    return x

_drawn_inputs = setup_inputs


def setup_inputs(seed=0):
    import zlib

    import numpy as np

    out = dict(_drawn_inputs(seed))
    spreads = {}
    factors = {}
    for name, (base, spread) in spreads.items():
        noise = np.random.default_rng([zlib.crc32(name.encode()), seed]).standard_normal(out[name].shape)
        drawn = base * np.exp(spread * noise) if base else spread * noise
        out[name] = jnp.asarray(drawn.astype(out[name].dtype))
    for name, factor in factors.items():
        out[name] = (out[name] * factor).astype(out[name].dtype)
    return out
```

```python
from contextlib import ExitStack

import concourse.bass as bass
from concourse import mybir

F32 = mybir.dt.float32
BF16 = mybir.dt.bfloat16
F16 = mybir.dt.float16
I32 = mybir.dt.int32
U32 = mybir.dt.uint32
ALU = mybir.AluOpType
ACT = mybir.ActivationFunctionType
AX = mybir.AxisListType

P = 128
LN_EPS = 1e-5
ROUTED_SCALE = 2.5
W_SCALE = 256.0
G_SCALE = 16.0
QH = 32
TOP_K = 2


def xattn_ffn_kernel(nc, x, ctx_in, gate_w, w1, w2, w3, sw1, sw2, sw3, out):
    B, S, D = x.shape
    C = ctx_in.shape[2]
    E, _, H = w1.shape
    HD = D // QH
    KV = C // HD
    G = QH // KV
    ST = S // P
    N = B * S
    NT = N // P
    DC = D // P
    XC = D + C
    BLK = XC // P
    HC = -(-H // P)
    HL = H - (HC - 1) * P
    RT = (N * TOP_K) // P + E
    TILES = NT + RT
    SLOTS = TILES * P
    ROW = D + 4
    NPART = 3
    QP = (0, 1, 2, 0, 1, 0)
    KP = (0, 0, 0, 1, 1, 2)
    KR = HD * len(QP)
    NSLOT = 4
    UN = KV
    LOADS = 16 * (len(QP) + len(KP) + 1)
    SCALE = float(HD) ** -0.5
    assert HD == 16 and ST == 4 and G == 4 and UN % NSLOT == 0 and KR == 96 and TILES % 2 == 0

    x_rows = x.rearrange("b s d -> (b s) d")
    ctx_rows = ctx_in.rearrange("b s d -> (b s) d")
    out_rows = out.rearrange("b s d -> (b s) d")

    parts_d = nc.dram_tensor("parts_scratch", (NPART, B, XC, S), BF16).ap()
    attn_d = nc.dram_tensor("attn_scratch", ((B + 1) * S, D), F32).ap()
    x1_d = nc.dram_tensor("x1_scratch", (N, D), F32).ap()
    xs_d = nc.dram_tensor("slots_in_scratch", (SLOTS, ROW), F32).ap()
    ys_d = nc.dram_tensor("slots_out_scratch", (SLOTS, D), F32).ap()

    with ExitStack() as whole:
        def sb(stack, name, shape, dt):
            return stack.enter_context(nc.sbuf_tensor(name, shape, dt))

        def pb(stack, name, shape, dt):
            return stack.enter_context(nc.psum_tensor(name, shape, dt))

        def sem(stack, name):
            return stack.enter_context(nc.semaphore(name))

        W13 = sb(whole, "W13", [P, E + 1, DC, 2, 2 * H], F16)
        W2 = sb(whole, "W2", [P, E + 1, HC, 2, D], F16)
        identf = sb(whole, "identf", [P, P], F32)

        with ExitStack() as st:
            identb = sb(st, "identb", [P, P], BF16)
            xin = sb(st, "xin", [P, ST, XC], F32)
            bst = sb(st, "bst", [P, ST, 6], F32)
            mv = sb(st, "mv", [P, ST, 2], F32)
            veps = sb(st, "veps", [P, ST], F32)
            sdev = sb(st, "sdev", [P, ST], F32)
            rstd = sb(st, "rstd", [P, ST], F32)
            part = sb(st, "part", [P, 2, NPART, XC], BF16)
            rest = sb(st, "rest", [P, 2, XC], F32)
            stage = sb(st, "stage", [P, NPART, BLK, S], BF16)
            psT = [pb(st, f"psT{i}", [P, BLK, P], BF16) for i in range(2 * NPART)]
            s_id = sem(st, "a_ident")
            s_xin = [sem(st, f"a_xin{i}") for i in range(ST)]
            s_bst, s_mv, s_veps, s_sdev, s_rstd = (sem(st, f"a_{n}") for n in ("bst", "mv", "veps", "sdev", "rstd"))
            s_xn = sem(st, "a_xn")
            s_rest = sem(st, "a_rest")
            s_part = [sem(st, f"a_part{i}") for i in range(NPART)]
            s_turned = [sem(st, f"a_turned{i}") for i in range(NPART)]
            s_evac = [sem(st, f"a_evac{i}") for i in range(NPART)]
            s_stored = sem(st, "a_stored")

            with nc.Block() as block:
                @block.sync
                def _(sp):
                    def load(b, t):
                        at = bass.ds(b * S + t * P, P)
                        sp.dma_start(xin[:, t, 0:D], x_rows[at, :]).then_inc(s_xin[t], 16)
                        sp.dma_start(xin[:, t, D:XC], ctx_rows[at, :]).then_inc(s_xin[t], 16)

                    def step(b, last):
                        if not last:
                            for t in range(ST):
                                sp.wait_ge(s_rest, ST * b + t + 1)
                                sp.wait_ge(s_part[0], ST * b + t + 1)
                                load(b + 1, t)
                        for a in range(NPART):
                            sp.wait_ge(s_evac[a], ST * b + ST)
                            sp.dma_start(parts_d[a, bass.ds(b, 1)].rearrange("o (k p) s -> p (o k) s", p=P),
                                         stage[:, a]).then_inc(s_stored, 16)

                    for t in range(ST):
                        load(0, t)
                    with sp.Fori(0, B - 1) as b:
                        step(b, False)
                    step(B - 1, True)
                    sp.wait_ge(s_stored, 16 * NPART * B)

                @block.gpsimd
                def _(pool):
                    nc.gpsimd.memset(identb[:], 0.0).then_inc(s_id, 1)
                    nc.gpsimd.memset(identf[:], 0.0).then_inc(s_id, 1)
                    pool.wait_ge(s_id, 2)
                    for m in (identb, identf):
                        nc.gpsimd.affine_select(out=m[:], in_=m[:], compare_op=ALU.not_equal, fill=1.0, base=0,
                                                pattern=[[-1, P]], channel_multiplier=1).then_inc(s_id, 1)

                @block.vector
                def _(dve):
                    with dve.Fori(0, B) as b:
                        def aggregate(t):
                            nc.vector.bn_aggr(mv[:, t], bst[:, t]).then_inc(s_mv, 1)

                        for t in range(ST):
                            dve.wait_ge(s_xin[t], 32 * b + 32)
                            if t >= 1:
                                dve.wait_ge(s_bst, ST * b + t)
                            nc.vector.bn_stats(bst[:, t], xin[:, t, 0:D]).then_inc(s_bst, 1)
                            if t >= 1:
                                aggregate(t - 1)
                        dve.wait_ge(s_bst, ST * b + ST)
                        dve.wait_ge(s_mv, ST * b + ST - 1)
                        nc.vector.tensor_scalar_add(veps[:, 0:ST - 1], mv[:, 0:ST - 1, 1], LN_EPS).then_inc(s_veps, 1)
                        aggregate(ST - 1)
                        dve.wait_ge(s_mv, ST * b + ST)
                        nc.vector.tensor_scalar_add(veps[:, ST - 1:ST], mv[:, ST - 1:ST, 1], LN_EPS).then_inc(s_veps, 1)
                        dve.wait_ge(s_sdev, b + 1)
                        nc.vector.reciprocal(rstd[:], sdev[:]).then_inc(s_rstd, 1)
                        dve.wait_ge(s_rstd, b + 1)

                        def norm(t):
                            nc.vector.tensor_scalar(xin[:, t, 0:D], xin[:, t, 0:D], mv[:, t, 0:1], rstd[:, t:t + 1],
                                                    ALU.subtract, ALU.mult).then_inc(s_xn, 1)

                        def first_rest(t):
                            dve.wait_ge(s_part[0], ST * b + t + 1)
                            nc.vector.tensor_tensor(rest[:, t % 2], xin[:, t], part[:, t % 2, 0],
                                                    ALU.subtract).then_inc(s_rest, 1)

                        def third_part(t):
                            dve.wait_ge(s_part[1], ST * b + t + 1)
                            nc.vector.tensor_tensor(part[:, t % 2, 2], rest[:, t % 2], part[:, t % 2, 1],
                                                    ALU.subtract).then_inc(s_part[2], 1)

                        def evac(t):
                            dve.wait_ge(s_turned[1], ST * b + t + 1)
                            nc.vector.tensor_copy(stage[:, 1, :, t * P:(t + 1) * P], psT[NPART * (t % 2) + 1][:])\
                                .then_inc(s_evac[1], 1)

                        for t in range(ST + 2):
                            if t < ST:
                                norm(t)
                                first_rest(t)
                            if 0 <= t - 1 < ST:
                                third_part(t - 1)
                            if 0 <= t - 2 < ST:
                                if t == 2:
                                    dve.wait_ge(s_stored, 16 * NPART * b)
                                evac(t - 2)

                @block.scalar
                def _(act):
                    with act.Fori(0, B) as b:
                        act.wait_ge(s_veps, 2 * b + 2)
                        nc.scalar.activation(sdev[:], veps[:], ACT.Sqrt).then_inc(s_sdev, 1)

                        def part0(t):
                            act.wait_ge(s_xn, ST * b + t + 1)
                            if t >= 2:
                                act.wait_ge(s_turned[0], ST * b + t - 1)
                            else:
                                act.wait_ge(s_turned[0], ST * b)
                            nc.scalar.activation(part[:, t % 2, 0], xin[:, t], ACT.Copy).then_inc(s_part[0], 1)

                        def part1(t):
                            act.wait_ge(s_rest, ST * b + t + 1)
                            nc.scalar.activation(part[:, t % 2, 1], rest[:, t % 2], ACT.Copy).then_inc(s_part[1], 1)

                        def evac(t, a):
                            act.wait_ge(s_turned[a], ST * b + t + 1)
                            nc.scalar.activation(stage[:, a, :, t * P:(t + 1) * P], psT[NPART * (t % 2) + a][:],
                                                 ACT.Copy).then_inc(s_evac[a], 1)

                        for t in range(ST + 1):
                            if t < ST:
                                part0(t)
                                part1(t)
                            if t >= 1:
                                if t == 1:
                                    act.wait_ge(s_stored, 16 * NPART * b)
                                evac(t - 1, 0)
                                evac(t - 1, 2)

                @block.tensor
                def _(pe):
                    pe.wait_ge(s_id, 4)
                    with pe.Fori(0, B) as b:
                        for t in range(ST):
                            for a in range(NPART):
                                pe.wait_ge(s_part[a], ST * b + t + 1)
                                if t >= 2:
                                    pe.wait_ge(s_evac[a], ST * b + t - 1)
                                else:
                                    pe.wait_ge(s_evac[a], ST * b)
                                for k in range(BLK):
                                    last = nc.tensor.transpose(psT[NPART * (t % 2) + a][:, k], part[:, t % 2, a, k * P:(k + 1) * P],
                                                               identb[:])
                                last.then_inc(s_turned[a], 1)

        with ExitStack() as st:
            qs = sb(st, "qs", [P, NSLOT, G, S], BF16)
            ks = sb(st, "ks", [P, NSLOT, S], BF16)
            va = sb(st, "va", [P, NSLOT, ST, 32], F32)
            pr = sb(st, "pr", [P, 2, G, S], F32)
            ot = sb(st, "ot", [P, S], F32)
            nmax = sb(st, "nmax", [P, 2, G * ST], F32)
            nrow = sb(st, "nrow", [G * ST, 2, P], BF16)
            rec = sb(st, "rec", [P, ST, G], F32)
            ob = sb(st, "ob", [P, 2, ST, G * HD], F32)
            wst = sb(st, "wst", [P, 2, DC * H], F32)
            w_scale = sb(st, "w_scale", [P, 1], F32)
            zrow = sb(st, "zrow", [P, ROW // 4], F32)
            psS = [pb(st, f"psS{i}", [P, 2, S], F32) for i in range(2)]
            psM = pb(st, "psM", [P, 2, S], F32)
            psO = pb(st, "psO", [P, S], F32)
            psX = pb(st, "psX", [P, ST, P], F32)

            s_init = sem(st, "b_init")
            s_load = [sem(st, f"b_load{i}") for i in range(NSLOT)]
            s_row = [sem(st, f"b_row{i}") for i in range(NSLOT)]
            s_store = [sem(st, f"b_store{i}") for i in range(2)]
            s_mscore, s_nmax, s_nmaxT, s_nrow = (sem(st, f"b_{n}") for n in ("mscore", "nmax", "nmaxT", "nrow"))
            s_score, s_exp, s_pv, s_ocopy, s_oT, s_rec, s_out = (
                sem(st, f"b_{n}") for n in ("score", "exp", "pv", "ocopy", "oT", "rec", "out"))
            s_w = [sem(st, f"b_w{i}") for i in range(2)]
            s_wsc, s_whi, s_wlo, s_zero, s_zd = (sem(st, f"b_{n}") for n in ("wsc", "whi", "wlo", "zero", "zd"))

            with nc.Block() as block:
                @block.sync
                def _(sp):
                    def load_unit(b, k):
                        n = k % NSLOT
                        b, k = b + k // UN, k % UN
                        for j, (qa, ka) in enumerate(zip(QP, KP)):
                            rows = slice(j * HD, (j + 1) * HD)
                            src = parts_d[qa, bass.ds(b, 1), k * G * HD:(k + 1) * G * HD, :]
                            sp.dma_start(qs[rows, n], src.rearrange("o (g d) s -> d (o g) s", g=G)).then_inc(s_load[n], 16)
                            src = parts_d[ka, bass.ds(b, 1), D + k * HD:D + (k + 1) * HD, :]
                            sp.dma_start(ks[rows, n], src.rearrange("o d s -> d (o s)")).then_inc(s_load[n], 16)
                        src = ctx_rows[bass.ds(b * S, S), k * HD:(k + 1) * HD]
                        sp.dma_start(va[:, n, :, 0:HD], src.rearrange("(t p) d -> p t d", p=P)).then_inc(s_load[n], 16)

                    def send_row(b, k):
                        n = k % NSLOT
                        sp.wait_ge(s_nrow, UN * b + k + 1)
                        sp.dma_start(qs[KR:KR + 1, n].rearrange("o g s -> o (g s)"), nrow[:, k % 2]).then_inc(s_row[n], 16)

                    def store(b, k):
                        kk = (k - 1) % UN
                        row0 = (b + (1 if k else 0)) * S
                        sp.wait_ge(s_out, UN * b + k + 1)
                        dst = attn_d[bass.ds(row0, S), kk * G * HD:(kk + 1) * G * HD]
                        sp.dma_start(dst.rearrange("(t p) c -> p t c", p=P), ob[:, k % 2]).then_inc(s_store[k % 2], 16)

                    def batch(b, last):
                        for k in range(UN):
                            if not last or k + 3 < UN:
                                sp.wait_ge(s_pv, 4 * (UN * b + k) + 2)
                                load_unit(b, k + 3)
                            store(b, k)
                            if not last or k + 1 < UN:
                                send_row(b, k + 1)

                    sp.wait_ge(s_init, 6)
                    for k in range(3):
                        load_unit(0, k)
                    send_row(0, 0)
                    with sp.Fori(0, B - 1) as b:
                        batch(b, False)
                    batch(B - 1, True)
                    store(B, 0)
                    sp.wait_ge(s_store[0], 16 * (UN * B // 2 + 1))
                    sp.wait_ge(s_store[1], 16 * (UN * B // 2))

                @block.tensor
                def _(pe):
                    def max_scores(b, k, j):
                        n, (t, g) = k % NSLOT, divmod(j, G)
                        u = UN * b + k
                        if j == 0:
                            pe.wait_ge(s_load[n], LOADS * (UN // NSLOT * b + k // NSLOT + 1))
                        if k >= 1 or j >= 2:
                            pe.wait_ge(s_nmax, 16 * u + j - 1)
                        nc.tensor.matmul(psM[:, j % 2], qs[0:KR, n, g, t * P:(t + 1) * P], ks[0:KR, n],
                                         start=True, stop=True).then_inc(s_mscore, 1)

                    def turn_max(b, k):
                        u = UN * b + k
                        pe.wait_ge(s_nmax, 16 * (u + 1))
                        if k >= 1:
                            pe.wait_ge(s_out, u)
                        nc.tensor.transpose(psX[0:G * ST, 0], nmax[:, k % 2], identf[:]).then_inc(s_nmaxT, 1)

                    def turn_out(b, k):
                        u = UN * b + k
                        pe.wait_ge(s_ocopy, u + 1)
                        pe.wait_ge(s_nrow, u + 1)
                        for t in range(ST):
                            last = nc.tensor.transpose(psX[:, t], ot[:, t * P:(t + 1) * P], identf[:])
                        last.then_inc(s_oT, 1)

                    def scores(b, k, t, h):
                        n, c = k % NSLOT, 2 * ST * (UN * b + k) + 2 * t + h
                        pe.wait_ge(s_exp, c + 1)
                        for g in range(2):
                            last = nc.tensor.matmul(psS[h][:, g], ks[0:KR + 1, n, t * P:(t + 1) * P],
                                                    qs[0:KR + 1, n, 2 * h + g], start=True, stop=True)
                        last.then_inc(s_score, 1)

                    def values(n, t):
                        for g in range(G):
                            last = nc.tensor.matmul(psO[32 * g:32 * g + 32], va[:, n, t], pr[:, t % 2, g],
                                                    start=(t == 0), stop=(t == ST - 1))
                        last.then_inc(s_pv, 1)

                    def batch(b, last):
                        for k in range(UN):
                            n = k % NSLOT
                            pe.wait_ge(s_row[n], 16 * (UN // NSLOT * b + k // NSLOT + 1))
                            for t in range(ST):
                                for h in range(2):
                                    scores(b, k, t, h)
                                    if not last or k + 2 < UN:
                                        for j in range(2):
                                            max_scores(b, k + 2, 4 * t + 2 * h + j)
                                if t == 0:
                                    pe.wait_ge(s_exp, 2 * ST * (UN * b + k) + 2)
                                    values((k - 1) % NSLOT, ST - 1)
                                    continue
                                if t == 1:
                                    turn_out(b, k)
                                pe.wait_ge(s_exp, 2 * ST * (UN * b + k) + 2 * t + 2)
                                values(n, t - 1)
                                if t == 2 and (not last or k + 1 < UN):
                                    turn_max(b, k + 1)

                    pe.wait_ge(s_init, 6)
                    values(NSLOT - 1, 0)
                    for j in range(G * ST):
                        max_scores(0, 0, j)
                    turn_max(0, 0)
                    for j in range(G * ST):
                        max_scores(0, 1, j)
                    with pe.Fori(0, B - 1) as b:
                        batch(b, False)
                    batch(B - 1, True)
                    pe.wait_ge(s_exp, 2 * ST * UN * B + 2)
                    values((UN - 1) % NSLOT, ST - 1)
                    pe.wait_ge(s_ocopy, UN * B + 1)
                    pe.wait_ge(s_out, UN * B)
                    for t in range(ST):
                        tail = nc.tensor.transpose(psX[:, t], ot[:, t * P:(t + 1) * P], identf[:])
                    tail.then_inc(s_oT, 1)

                @block.vector
                def _(dve):
                    def maximum(b, k, j):
                        u = UN * b + k
                        t, g = divmod(j, G)
                        if j == 0 and k >= 2:
                            dve.wait_ge(s_nmaxT, u - 1)
                        dve.wait_ge(s_mscore, 16 * u + j + 1)
                        nc.vector.tensor_reduce(nmax[:, k % 2, g * ST + t:g * ST + t + 1], psM[:, j % 2], AX.X, ALU.max,
                                                negate=True).then_inc(s_nmax, 1)

                    def row(b, k):
                        u = UN * b + k
                        dve.wait_ge(s_nmaxT, u + 1)
                        if k >= 2:
                            m = k - 2
                            dve.wait_ge(s_row[m % NSLOT], 16 * (UN // NSLOT * b + m // NSLOT + 1))
                        nc.vector.tensor_copy(nrow[:, k % 2], psX[0:G * ST, 0]).then_inc(s_nrow, 1)

                    def normalise(b, k):
                        u = UN * b + k
                        dve.wait_ge(s_oT, u + 1)
                        o = psX[:].rearrange("p t (g c) -> p t g c", g=G)
                        nc.vector.reciprocal(rec[:], o[:, :, :, HD]).then_inc(s_rec, 1)
                        dve.wait_ge(s_rec, u + 1)
                        dve.wait_ge(s_store[k % 2], 16 * (UN // 2 * b + k // 2))
                        nc.vector.tensor_tensor(ob[:, k % 2].rearrange("p t (g d) -> p t g d", g=G), o[:, :, :, 0:HD],
                                                rec[:].unsqueeze(3).to_broadcast([P, ST, G, HD]),
                                                ALU.mult).then_inc(s_out, 1)

                    def batch(b, last):
                        for k in range(UN):
                            ahead = not last or k + 2 < UN
                            for j in range(8):
                                if ahead:
                                    maximum(b, k + 2, j)
                            normalise(b, k)
                            for j in range(8, 12):
                                if ahead:
                                    maximum(b, k + 2, j)
                            if not last or k + 1 < UN:
                                row(b, k + 1)
                            for j in range(12, 16):
                                if ahead:
                                    maximum(b, k + 2, j)

                    nc.vector.memset(ks[KR:KR + 1], 1.0).then_inc(s_init, 1)
                    nc.vector.memset(va[:], 0.0).then_inc(s_init, 1)
                    nc.vector.memset(pr[:], 1.0).then_inc(s_init, 1)
                    dve.wait_ge(s_init, 3)
                    nc.vector.memset(va[:, :, :, HD:HD + 1], 1.0).then_inc(s_init, 3)
                    for j in range(G * ST):
                        maximum(0, 0, j)
                    row(0, 0)
                    for j in range(G * ST):
                        maximum(0, 1, j)
                    with dve.Fori(0, B - 1) as b:
                        batch(b, False)
                    batch(B - 1, True)
                    normalise(B, 0)

                @block.scalar
                def _(act):
                    def exps(b, k, t, h):
                        u = UN * b + k
                        act.wait_ge(s_score, 2 * ST * u + 2 * t + h + 1)
                        act.wait_ge(s_pv, ST * u + t + 1)
                        nc.scalar.activation(pr[:, t % 2, 2 * h:2 * h + 2], psS[h][:], ACT.Exp, scale=SCALE)\
                            .then_inc(s_exp, 1)

                    def copy_out(b, k):
                        u = UN * b + k
                        act.wait_ge(s_pv, ST * u + 2)
                        act.wait_ge(s_oT, u)
                        nc.scalar.activation(ot[:], psO[:], ACT.Copy).then_inc(s_ocopy, 1)

                    def batch(b):
                        for k in range(UN):
                            for t in range(ST):
                                for h in range(2):
                                    exps(b, k, t, h)
                                if t == 0:
                                    copy_out(b, k)

                    nc.scalar.activation(rec[:], identf[:, 0:ST * G].rearrange("p (t g) -> p t g", g=G), ACT.Copy).then_inc(s_exp, 2)
                    with act.Fori(0, B) as b:
                        batch(b)
                    copy_out(B, 0)

                @block.gpsimd
                def _(pool):
                    nc.gpsimd.memset(zrow[:], 0.0).then_inc(s_zero, 1)
                    nc.gpsimd.memset(wst[:], 0.0).then_inc(s_zero, 1)
                    nc.gpsimd.memset(w_scale[:], W_SCALE).then_inc(s_zero, 1)
                    pool.wait_ge(s_zero, 3)
                    for c in range(4):
                        pool.dma_start(xs_d[NT * P:SLOTS, c * ROW // 4:(c + 1) * ROW // 4].rearrange("(t p) c -> p t c", p=P),
                                       zrow[:].unsqueeze(1).to_broadcast([P, RT, ROW // 4])).then_inc(s_zd, 16)

                    def split(i, src, hi, lo):
                        c = w_scale[0:src.shape[0]]
                        if len(src.shape) == 3:
                            c = c.unsqueeze(2)
                        c = c.to_broadcast(list(src.shape))
                        nc.gpsimd.tensor_tensor(hi, src, c, ALU.mult).then_inc(s_whi, 1)
                        nc.gpsimd.tensor_tensor(src, src, c, ALU.mult).then_inc(s_wsc, 1)
                        pool.wait_ge(s_whi, i + 1)
                        pool.wait_ge(s_wsc, i + 1)
                        nc.gpsimd.tensor_tensor(lo, src, hi, ALU.subtract).then_inc(s_wlo, 1)

                    def expert(e, w1e, w3e, w2e, slot):
                        full = (HC - 1) * P
                        for half, w in enumerate((w1e, w3e)):
                            pool.wait_ge(s_zero, 3)
                            pool.wait_ge(s_wlo, 4 * e)
                            src = wst[:, half].rearrange("p (c h) -> p c h", h=H)
                            pool.dma_start(src, w.rearrange("(c p) h -> p c h", p=P)).then_inc(s_w[half], 16)
                        for half in range(2):
                            pool.wait_ge(s_w[half], 32 * e + 16)
                            dst = W13[:, slot, :, :, half * H:(half + 1) * H]
                            split(4 * e + half, wst[:, half].rearrange("p (c h) -> p c h", h=H),
                                  fold(dst[..., 0, :]), fold(dst[..., 1, :]))
                        pool.wait_ge(s_zero, 3)
                        pool.wait_ge(s_wlo, 4 * e + 2)
                        pool.dma_start(wst[:, 0, 0:(HC - 1) * D].rearrange("p (c d) -> p c d", d=D),
                                       w2e[0:full].rearrange("(c p) d -> p c d", p=P)).then_inc(s_w[0], 16)
                        pool.dma_start(wst[0:HL, 1, 0:D], w2e[full:H]).then_inc(s_w[1], 16)
                        pool.wait_ge(s_w[0], 32 * e + 32)
                        split(4 * e + 2, wst[:, 0, 0:(HC - 1) * D].rearrange("p (c d) -> p c d", d=D),
                              fold(W2[:, slot, 0:HC - 1, 0]), fold(W2[:, slot, 0:HC - 1, 1]))
                        pool.wait_ge(s_w[1], 32 * e + 32)
                        split(4 * e + 3, wst[0:HL, 1:2, 0:D], fold(W2[0:HL, slot, HC - 1:HC, 0]),
                              fold(W2[0:HL, slot, HC - 1:HC, 1]))

                    def fold(ap):
                        return ap.squeeze(1) if len(ap.shape) == 4 else ap

                    expert(0, sw1, sw3, sw2, E)
                    with pool.Fori(0, E) as e:
                        one = bass.ds(e, 1)
                        expert(e + 1, w1[one].squeeze(0), w3[one].squeeze(0), w2[one].squeeze(0), one)
                    pool.wait_ge(s_wlo, 4 * (E + 1))
                    pool.wait_ge(s_zd, 64)

        with ExitStack() as st_cd:
            slot_i = sb(st_cd, "slot_i", [P, TOP_K, NT], I32)
            tile_e = sb(st_cd, "tile_e", [P, TILES], I32)
            with ExitStack() as st:
                xr = sb(st, "xr", [P, NT, ROW], F32)
                ld = sb(st, "ld", [P, 2, D], F32)
                bst = sb(st, "bst2", [P, NT, 6], F32)
                mv = sb(st, "mv2", [P, NT, 2], F32)
                veps = sb(st, "veps2", [P, NT], F32)
                sdev = sb(st, "sdev2", [P, NT], F32)
                rstd = sb(st, "rstd2", [P, NT], F32)
                xT = sb(st, "xT", [P, 2, DC, P], F32)
                gw = sb(st, "gw", [E, D], F32)
                gwT = sb(st, "gwT", [P, DC, E], F32)
                sc = sb(st, "sc", [P, NT, E], F32)
                mx = sb(st, "mx", [P, NT, 8], F32)
                ix = sb(st, "ix", [P, NT, 8], U32)
                ixf = sb(st, "ixf", [P, NT, TOP_K], F32)
                iota_e = sb(st, "iota_e", [P, NT, E], F32)
                iota_t = sb(st, "iota_t", [P, RT], F32)
                before = sb(st, "before", [P, P], F32)
                ones = sb(st, "ones", [P, P], F32)
                pick = sb(st, "pick", [P, TOP_K, NT, E], F32)
                both = sb(st, "both", [P, NT, E], F32)
                cum = sb(st, "cum", [P, NT + 1, E], F32)
                tot = sb(st, "tot", [P, NT, E], F32)
                cnt_i = sb(st, "cnt_i", [P, 3, E], I32)
                padf = sb(st, "padf", [P, E], F32)
                base = sb(st, "base", [P, E + 1], F32)
                slots = sb(st, "slots", [P, NT, E], F32)
                hit = sb(st, "hit", [P, NT, E], F32)
                slotf = sb(st, "slotf", [P, TOP_K, NT], F32)
                den = sb(st, "den", [P, 2, NT], F32)
                wts = sb(st, "wts", [P, TOP_K, NT], F32)
                past = sb(st, "past", [P, RT, E], F32)
                tef = sb(st, "tef", [P, TILES], F32)
                psT = [pb(st, f"psT2{i}", [P, DC, P], F32) for i in range(2)]
                psL = pb(st, "psL", [P, NT, E], F32)
                psC = [pb(st, f"psC{i}", [P, NT, E], F32) for i in range(2)]
                psG = pb(st, "psG", [P, DC, E], F32)

                s_lx = sem(st, "c_lx")
                s_la = [sem(st, f"c_la{i}") for i in range(2)]
                s_gw = sem(st, "c_gw")
                s_cst, s_gT, s_gwT, s_x1, s_x1d, s_bst, s_mv, s_veps, s_sdev, s_rstd, s_xn = (
                    sem(st, f"c_{n}") for n in ("cst", "gT", "gwT", "x1", "x1d", "bst", "mv", "veps", "sdev", "rstd", "xn"))
                s_xTp, s_xT, s_log, s_sc, s_both, s_count, s_v, s_ready, s_shw, s_shd, s_sent, s_w2nd, s_te = (
                    sem(st, f"c_{n}") for n in ("xTp", "xT", "log", "sc", "both", "count", "v", "ready", "shw", "shd",
                                                "sent", "w2nd", "te"))

                with nc.Block() as block:
                    @block.sync
                    def _(sp):
                        sp.dma_start(gw[:], gate_w).then_inc(s_gw, 16)
                        sp.dma_start(xr[:, :, 0:D], x_rows.rearrange("(t p) d -> p t d", p=P)).then_inc(s_lx, 16)
                        for t in range(NT):
                            if t >= 2:
                                sp.wait_ge(s_x1, t - 1)
                            sp.dma_start(ld[:, t % 2], attn_d[S + t * P:S + (t + 1) * P]).then_inc(s_la[t % 2], 16)
                        sp.wait_ge(s_x1, NT)
                        sp.dma_start(x1_d.rearrange("(t p) d -> p t d", p=P), xr[:, :, 0:D]).then_inc(s_x1d, 16)
                        sp.wait_ge(s_xn, NT)
                        sp.wait_ge(s_shw, 1)
                        sp.dma_start(xs_d[0:N].rearrange("(t p) d -> p t d", p=P), xr[:]).then_inc(s_shd, 16)
                        sp.wait_ge(s_shd, 16)

                    @block.gpsimd
                    def _(pool):
                        nc.gpsimd.iota(iota_e[:], [[0, NT], [1, E]], base=0, channel_multiplier=0,
                                       allow_small_or_imprecise_dtypes=True).then_inc(s_cst, 1)
                        nc.gpsimd.iota(iota_t[:], [[P, RT]], base=0, channel_multiplier=0,
                                       allow_small_or_imprecise_dtypes=True).then_inc(s_cst, 1)
                        nc.gpsimd.memset(ones[:], 1.0).then_inc(s_cst, 1)
                        pool.wait_ge(s_cst, 3)
                        nc.gpsimd.affine_select(out=before[:], in_=ones[:], compare_op=ALU.is_gt, fill=0.0, base=0,
                                                pattern=[[1, P]], channel_multiplier=-1).then_inc(s_cst, 1)
                        for k in range(TOP_K):
                            pool.wait_ge(s_ready if k == 0 else s_w2nd, 1)
                            for t in range(NT):
                                nc.gpsimd.indirect_dma_start(
                                    out=xs_d, out_offset=bass.IndirectOffsetOnAxis(ap=slot_i[:, k, t:t + 1], axis=0),
                                    in_=xr[:, t], in_offset=None).then_inc(s_sent, 16)
                            pool.wait_ge(s_sent, 16 * NT * (k + 1))

                    @block.scalar
                    def _(act):
                        act.wait_ge(s_veps, 1)
                        nc.scalar.activation(sdev[:], veps[:], ACT.Sqrt).then_inc(s_sdev, 1)
                        for t in range(NT):
                            act.wait_ge(s_xTp, t + 1)
                            if t >= 2:
                                act.wait_ge(s_log, t - 1)
                            nc.scalar.activation(xT[:, t % 2], psT[t % 2][:], ACT.Copy).then_inc(s_xT, 1)
                        act.wait_ge(s_log, NT)
                        nc.scalar.activation(sc[:], psL[:], ACT.Sigmoid).then_inc(s_sc, 1)

                    @block.tensor
                    def _(pe):
                        pe.wait_ge(s_gw, 16)
                        for c in range(DC):
                            last = nc.tensor.transpose(psG[:, c], gw[:, c * P:(c + 1) * P], identf[0:E, 0:E])
                        last.then_inc(s_gT, 1)
                        pe.wait_ge(s_gwT, 1)

                        def logits(t):
                            pe.wait_ge(s_xT, t + 1)
                            for c in range(DC):
                                last = nc.tensor.matmul(psL[:, t], xT[:, t % 2, c], gwT[:, c], start=(c == 0), stop=(c == DC - 1))
                            last.then_inc(s_log, 1)

                        for t in range(NT):
                            pe.wait_ge(s_xn, t + 1)
                            if t >= 2:
                                pe.wait_ge(s_xT, t - 1)
                            for c in range(DC):
                                last = nc.tensor.transpose(psT[t % 2][:, c], xr[:, t, c * P:(c + 1) * P], identf[:])
                            last.then_inc(s_xTp, 1)
                            if t >= 1:
                                logits(t - 1)
                        logits(NT - 1)
                        pe.wait_ge(s_cst, 4)
                        pe.wait_ge(s_both, 1)
                        nc.tensor.matmul(psC[0][:].rearrange("p t e -> p (t e)"), before[:],
                                         both[:].rearrange("p t e -> p (t e)"), start=True, stop=True)
                        nc.tensor.matmul(psC[1][:].rearrange("p t e -> p (t e)"), ones[:],
                                         both[:].rearrange("p t e -> p (t e)"), start=True, stop=True).then_inc(s_count, 1)

                    @block.vector
                    def _(dve):
                        steps = [0]

                        def then(ins):
                            steps[0] += 1
                            ins.then_inc(s_v, 1)
                            dve.wait_ge(s_v, steps[0])

                        dve.wait_ge(s_gT, 1)
                        nc.vector.tensor_copy(gwT[:], psG[:]).then_inc(s_gwT, 1)
                        dve.wait_ge(s_lx, 16)
                        for t in range(NT):
                            dve.wait_ge(s_la[t % 2], 16 * (t // 2 + 1))
                            nc.vector.tensor_tensor(xr[:, t, 0:D], xr[:, t, 0:D], ld[:, t % 2], ALU.add).then_inc(s_x1, 1)
                            dve.wait_ge(s_x1, t + 1)
                            nc.vector.bn_stats(bst[:, t], xr[:, t, 0:D]).then_inc(s_bst, 1)
                        for t in range(NT):
                            dve.wait_ge(s_bst, t + 1)
                            nc.vector.bn_aggr(mv[:, t], bst[:, t]).then_inc(s_mv, 1)
                        dve.wait_ge(s_mv, NT)
                        nc.vector.tensor_scalar_add(veps[:], mv[:, :, 1], LN_EPS).then_inc(s_veps, 1)
                        dve.wait_ge(s_sdev, 1)
                        then(nc.vector.reciprocal(rstd[:], sdev[:]))
                        nc.vector.memset(xr[:, :, D:ROW], 1.0 / (W_SCALE * G_SCALE)).then_inc(s_shw, 1)
                        dve.wait_ge(s_x1d, 16)
                        for t in range(NT):
                            nc.vector.tensor_scalar(xr[:, t, 0:D], xr[:, t, 0:D], mv[:, t, 0:1], rstd[:, t:t + 1],
                                                    ALU.subtract, ALU.mult).then_inc(s_xn, 1)
                        dve.wait_ge(s_sc, 1)
                        for t in range(NT):
                            last = nc.vector.max(mx[:, t], sc[:, t])
                        then(last)
                        for t in range(NT):
                            last = nc.vector.max_index(ix[:, t], mx[:, t], sc[:, t])
                        then(last)
                        then(nc.vector.tensor_copy(ixf[:], ix[:, :, 0:TOP_K]))
                        dve.wait_ge(s_cst, 4)
                        for k in range(TOP_K):
                            then(nc.vector.tensor_tensor(pick[:, k], iota_e[:], ixf[:, :, k:k + 1].to_broadcast([P, NT, E]),
                                                         ALU.is_equal))
                        nc.vector.tensor_tensor(both[:], pick[:, 0], pick[:, 1], ALU.add).then_inc(s_both, 1)
                        then(nc.vector.tensor_tensor(den[:, 0], mx[:, :, 0], mx[:, :, 1], ALU.add))
                        then(nc.vector.tensor_scalar_add(den[:, 0], den[:, 0], 1e-20))
                        then(nc.vector.reciprocal(den[:, 1], den[:, 0]))
                        for k in range(TOP_K):
                            then(nc.vector.tensor_tensor(wts[:, k], mx[:, :, k], den[:, 1], ALU.mult))
                        then(nc.vector.tensor_scalar_mul(wts[:], wts[:], ROUTED_SCALE / (W_SCALE * G_SCALE)))
                        dve.wait_ge(s_count, 1)
                        then(nc.vector.tensor_copy(tot[:], psC[1][:]))
                        then(nc.vector.memset(cum[:, 0], 0.0))
                        for t in range(NT):
                            then(nc.vector.tensor_tensor(cum[:, t + 1], cum[:, t], tot[:, t], ALU.add))
                        then(nc.vector.tensor_scalar_add(padf[:], cum[:, NT], float(P - 1)))
                        then(nc.vector.tensor_copy(cnt_i[:, 0], padf[:]))
                        then(nc.vector.tensor_single_scalar(cnt_i[:, 1], cnt_i[:, 0], P.bit_length() - 1, ALU.arith_shift_right))
                        then(nc.vector.tensor_copy(padf[:], cnt_i[:, 1]))
                        then(nc.vector.tensor_scalar_mul(padf[:], padf[:], float(P)))
                        then(nc.vector.memset(base[:, 0:1], 0.0))
                        for e in range(E):
                            then(nc.vector.tensor_tensor(base[:, e + 1:e + 2], base[:, e:e + 1], padf[:, e:e + 1], ALU.add))
                        then(nc.vector.tensor_tensor(slots[:], cum[:, 0:NT], psC[0][:], ALU.add))
                        then(nc.vector.tensor_tensor(slots[:], slots[:], base[:, 0:E].unsqueeze(1).to_broadcast([P, NT, E]), ALU.add))
                        for k in range(TOP_K):
                            then(nc.vector.tensor_tensor(hit[:], slots[:], pick[:, k], ALU.mult))
                            then(nc.vector.tensor_reduce(slotf[:, k], hit[:], AX.X, ALU.add))
                        then(nc.vector.tensor_scalar_add(slotf[:], slotf[:], float(N)))
                        then(nc.vector.tensor_copy(slot_i[:], slotf[:]))
                        dve.wait_ge(s_shd, 16)
                        nc.vector.tensor_copy(xr[:, :, D:D + 1], wts[:, 0].unsqueeze(2)).then_inc(s_ready, 1)
                        then(nc.vector.tensor_tensor(past[:], iota_t[:].unsqueeze(2).to_broadcast([P, RT, E]),
                                                     base[:, 1:E + 1].unsqueeze(1).to_broadcast([P, RT, E]), ALU.is_ge))
                        then(nc.vector.memset(tef[:, 0:NT], float(E)))
                        then(nc.vector.tensor_reduce(tef[:, NT:TILES], past[:], AX.X, ALU.add))
                        then(nc.vector.tensor_scalar_min(tef[:, NT:TILES], tef[:, NT:TILES], float(E - 1)))
                        nc.vector.tensor_copy(tile_e[:], tef[:]).then_inc(s_te, 1)
                        dve.wait_ge(s_sent, 16 * NT)
                        nc.vector.tensor_copy(xr[:, :, D:D + 1], wts[:, 1].unsqueeze(2)).then_inc(s_w2nd, 1)

            with ExitStack() as st:
                xt = sb(st, "xt", [P, 2, ROW], F32)
                xh = sb(st, "xh", [P, 2, DC, P], F16)
                xl = sb(st, "xl", [P, 2, DC, P], F16)
                sg = sb(st, "sg", [P, 2, H], F32)
                gg = sb(st, "gg", [P, 2, HC * P], F32)
                gh = sb(st, "gh", [P, 2, HC, P], F16)
                gl = sb(st, "gl", [P, 2, HC, P], F16)
                yo = sb(st, "yo", [P, 2, D], F32)
                wtc = sb(st, "wtc", [P, 2, 1], F32)
                psXT = pb(st, "psXT", [P, DC, P], F32)
                psH = pb(st, "psH", [P, 512], F32)
                psU = pb(st, "psU", [P, 512], F32)
                psGT = pb(st, "psGT", [P, HC, P], F32)
                psY = [pb(st, f"psY{i}", [P, D], F32) for i in range(2)]
                s_init = sem(st, "d_init")
                s_xt = [sem(st, f"d_xt{i}") for i in range(2)]
                s_yst = [sem(st, f"d_yst{i}") for i in range(2)]
                s_xT, s_xh, s_xl, s_hu, s_sg, s_g, s_gT, s_gh, s_gl, s_y, s_yo, s_wt = (
                    sem(st, f"d_{n}") for n in ("xT", "xh", "xl", "hu", "sg", "g", "gT", "gh", "gl", "y", "yo", "wt"))

                with nc.Block() as block:
                    @block.sync
                    def _(sp):
                        def load(i, j):
                            sp.dma_start(xt[:, j], xs_d[bass.ds(i * P, P), :]).then_inc(s_xt[j], 16)

                        def store(i, j):
                            sp.wait_ge(s_yo, i + 1)
                            sp.dma_start(ys_d[bass.ds(i * P, P), :], yo[:, j]).then_inc(s_yst[j], 16)

                        load(0, 0)
                        load(1, 1)
                        with sp.Fori(0, TILES // 2 - 1) as m:
                            for j in range(2):
                                sp.wait_ge(s_xT, 2 * m + j + 1)
                                sp.wait_ge(s_wt, 2 * m + j + 1)
                                load(2 * m + j + 2, j)
                                store(2 * m + j, j)
                        for j in range(2):
                            store(TILES - 2 + j, j)
                        for j in range(2):
                            sp.wait_ge(s_yst[j], 16 * (TILES // 2))

                    @block.tensor
                    def _(pe):
                        def turn_x(i, j, half):
                            pe.wait_ge(s_xt[j], 16 * half + 16)
                            pe.wait_ge(s_xh, i)
                            pe.wait_ge(s_xl, i)
                            for c in range(DC):
                                last = nc.tensor.transpose(psXT[:, c], xt[:, j, c * P:(c + 1) * P], identf[:])
                            last.then_inc(s_xT, 1)

                        def up(i, j):
                            e = pe.value_load(tile_e[0:1, bass.ds(i, 1)], min_val=0, max_val=E)
                            pe.wait_ge(s_xh, i + 1)
                            pe.wait_ge(s_xl, i + 1)
                            pe.wait_ge(s_g, i)
                            n = 0
                            for c in range(DC):
                                for xp, wp in ((xh, 0), (xh, 1), (xl, 0)):
                                    for ps, at in ((psH, 0), (psU, H)):
                                        last = nc.tensor.matmul(
                                            ps[:, 0:H], xp[:, j, c],
                                            W13[:, bass.ds(e, 1), c, wp, at:at + H].rearrange("p o h -> p (o h)"),
                                            start=(n == 0), stop=(n == 3 * DC - 1))
                                    n += 1
                            last.then_inc(s_hu, 1)
                            return e

                        def turn_g(i, j):
                            pe.wait_ge(s_g, i + 1)
                            pe.wait_ge(s_gh, i)
                            pe.wait_ge(s_gl, i)
                            for c in range(HC):
                                last = nc.tensor.transpose(psGT[:, c], gg[:, j, c * P:(c + 1) * P], identf[:])
                            last.then_inc(s_gT, 1)

                        def down(i, j):
                            e = pe.value_load(tile_e[0:1, bass.ds(i, 1)], min_val=0, max_val=E)
                            pe.wait_ge(s_gh, i + 1)
                            pe.wait_ge(s_gl, i + 1)
                            if not isinstance(i, int) or i >= 2:
                                pe.wait_ge(s_yo, i - 1)
                            n = 0
                            for c in range(HC):
                                rows = P if c < HC - 1 else HL
                                for gp, wp in ((gh, 0), (gh, 1), (gl, 0)):
                                    last = nc.tensor.matmul(
                                        psY[j][:], gp[0:rows, j, c],
                                        W2[0:rows, bass.ds(e, 1), c, wp, :].rearrange("p o d -> p (o d)"),
                                        start=(n == 0), stop=(n == 3 * HC - 1))
                                    n += 1
                            last.then_inc(s_y, 1)

                        turn_x(0, 0, 0)
                        up(0, 0)
                        turn_x(1, 1, 0)
                        turn_g(0, 0)
                        up(1, 1)
                        turn_x(2, 0, 1)
                        down(0, 0)
                        turn_g(1, 1)
                        up(2, 0)
                        turn_x(3, 1, 1)
                        down(1, 1)
                        turn_g(2, 0)
                        with pe.Fori(0, TILES // 2 - 2) as m:
                            up(2 * m + 3, 1)
                            turn_x(2 * m + 4, 0, m + 2)
                            down(2 * m + 2, 0)
                            turn_g(2 * m + 3, 1)
                            up(2 * m + 4, 0)
                            turn_x(2 * m + 5, 1, m + 2)
                            down(2 * m + 3, 1)
                            turn_g(2 * m + 4, 0)
                        up(TILES - 1, 1)
                        down(TILES - 2, 0)
                        turn_g(TILES - 1, 1)
                        down(TILES - 1, 1)

                    @block.scalar
                    def _(act):
                        def split_x(i, j):
                            act.wait_ge(s_xT, i + 1)
                            if not isinstance(i, int) or i >= 2:
                                act.wait_ge(s_hu, i - 1)
                            nc.scalar.activation(xh[:, j], psXT[:], ACT.Copy).then_inc(s_xh, 1)

                        def silu(i, j):
                            act.wait_ge(s_hu, i + 1)
                            nc.scalar.activation(sg[:, j], psH[:, 0:H], ACT.Silu, scale=1.0 / W_SCALE).then_inc(s_sg, 1)

                        def split_g(i, j):
                            act.wait_ge(s_gT, i + 1)
                            if not isinstance(i, int) or i >= 2:
                                act.wait_ge(s_y, i - 1)
                            nc.scalar.activation(gh[:, j], psGT[:], ACT.Copy).then_inc(s_gh, 1)

                        def tile(i, j, last=False):
                            silu(i, j)
                            if not last:
                                split_x(i + 1, 1 - j)
                            split_g(i, j)

                        split_x(0, 0)
                        tile(0, 0)
                        tile(1, 1)
                        with act.Fori(1, TILES // 2 - 1) as m:
                            tile(2 * m, 0)
                            tile(2 * m + 1, 1)
                        tile(TILES - 2, 0)
                        tile(TILES - 1, 1, last=True)

                    @block.vector
                    def _(dve):
                        def split_x(i, j):
                            dve.wait_ge(s_xh, i + 1)
                            nc.vector.tensor_tensor(xl[:, j], psXT[:], xh[:, j], ALU.subtract).then_inc(s_xl, 1)

                        def gate(i, j):
                            dve.wait_ge(s_sg, i + 1)
                            if not isinstance(i, int) or i >= 2:
                                dve.wait_ge(s_gT, i - 1)
                            nc.vector.scalar_tensor_tensor(gg[:, j, 0:H], psU[:, 0:H], G_SCALE / W_SCALE, sg[:, j],
                                                           ALU.mult, ALU.mult).then_inc(s_g, 1)

                        def split_g(i, j):
                            dve.wait_ge(s_gh, i + 1)
                            nc.vector.tensor_tensor(gl[:, j], psGT[:], gh[:, j], ALU.subtract).then_inc(s_gl, 1)

                        def weight(i, j, half):
                            dve.wait_ge(s_xt[j], 16 * half + 16)
                            if not isinstance(i, int) or i >= 2:
                                dve.wait_ge(s_yo, i - 1)
                            nc.vector.tensor_copy(wtc[:, j], xt[:, j, D:D + 1]).then_inc(s_wt, 1)

                        def result(i, j, half):
                            dve.wait_ge(s_y, i + 1)
                            dve.wait_ge(s_yst[j], 16 * half)
                            nc.vector.tensor_scalar_mul(yo[:, j], psY[j][:], wtc[:, j]).then_inc(s_yo, 1)

                        def tile(i, j, half, first=False, last=False):
                            gate(i, j)
                            if not last:
                                split_x(i + 1, 1 - j)
                            if not first:
                                result(i - 1, 1 - j, half if j else half - 1)
                            if not last:
                                weight(i + 1, 1 - j, half + 1 if j else half)
                            split_g(i, j)

                        nc.vector.memset(gg[:], 0.0).then_inc(s_init, 1)
                        dve.wait_ge(s_init, 1)
                        split_x(0, 0)
                        weight(0, 0, 0)
                        tile(0, 0, 0, first=True)
                        tile(1, 1, 0)
                        with dve.Fori(1, TILES // 2 - 1) as m:
                            tile(2 * m, 0, m)
                            tile(2 * m + 1, 1, m)
                        tile(TILES - 2, 0, TILES // 2 - 1)
                        tile(TILES - 1, 1, TILES // 2 - 1, last=True)
                        result(TILES - 1, 1, TILES // 2 - 1)

            with ExitStack() as st:
                NB = 3
                xb = sb(st, "xb", [P, NB, D], F32)
                yb = sb(st, "yb", [P, NB, D], F32)
                rb = sb(st, "rb", [P, NB, TOP_K, D], F32)
                s_in = [sem(st, f"e_in{i}") for i in range(NB)]
                s_g = [sem(st, f"e_g{i}") for i in range(NB)]
                s_o = [sem(st, f"e_o{i}") for i in range(NB)]
                s_a, s_b, s_c = (sem(st, f"e_{n}") for n in ("a", "b", "c"))
                with nc.Block() as block:
                    @block.sync
                    def _(sp):
                        def load(t):
                            n = t % NB
                            if t >= NB:
                                sp.wait_ge(s_o[n], 16 * (t // NB))
                            sp.dma_start(xb[:, n], x1_d[t * P:(t + 1) * P]).then_inc(s_in[n], 16)
                            sp.dma_start(yb[:, n], ys_d[t * P:(t + 1) * P]).then_inc(s_in[n], 16)

                        for t in range(NT):
                            load(t)
                            if t >= 2:
                                sp.wait_ge(s_c, t - 1)
                                sp.dma_start(out_rows[(t - 2) * P:(t - 1) * P], xb[:, (t - 2) % NB]).then_inc(s_o[(t - 2) % NB], 16)
                        for t in range(NT - 2, NT):
                            sp.wait_ge(s_c, t + 1)
                            sp.dma_start(out_rows[t * P:(t + 1) * P], xb[:, t % NB]).then_inc(s_o[t % NB], 16)
                        for n in range(NB):
                            sp.wait_ge(s_o[n], 16 * len(range(n, NT, NB)))

                    @block.gpsimd
                    def _(pool):
                        for t in range(NT):
                            n = t % NB
                            if t >= NB:
                                pool.wait_ge(s_c, t - NB + 1)
                            for k in range(TOP_K):
                                nc.gpsimd.indirect_dma_start(
                                    out=rb[:, n, k], out_offset=None, in_=ys_d,
                                    in_offset=bass.IndirectOffsetOnAxis(ap=slot_i[:, k, t:t + 1], axis=0)).then_inc(s_g[n], 16)

                    @block.vector
                    def _(dve):
                        for t in range(NT):
                            n = t % NB
                            dve.wait_ge(s_in[n], 32 * (t // NB + 1))
                            nc.vector.tensor_tensor(xb[:, n], xb[:, n], yb[:, n], ALU.add).then_inc(s_a, 1)
                            dve.wait_ge(s_g[n], 32 * (t // NB + 1))
                            nc.vector.tensor_tensor(rb[:, n, 0], rb[:, n, 0], rb[:, n, 1], ALU.add).then_inc(s_b, 1)
                            dve.wait_ge(s_a, t + 1)
                            dve.wait_ge(s_b, t + 1)
                            nc.vector.tensor_tensor(xb[:, n], xb[:, n], rb[:, n, 0], ALU.add).then_inc(s_c, 1)


_INS = ["x", "ctx_512", "L0_ffn_gate_w", "L0_ffn_w1", "L0_ffn_w2", "L0_ffn_w3", "L0_ffn_sw1", "L0_ffn_sw2", "L0_ffn_sw3"]


def kernel(**inputs):
    import numpy as _np
    import concourse.bacc as _bacc
    from concourse import mybir as _mybir
    from concourse.bass_utils import run_bass_kernel_spmd as _run

    nc = _bacc.Bacc("TRN2", target_bir_lowering=False, num_devices=1)
    arrays, args = {}, []
    for name in _INS:
        a = _np.ascontiguousarray(inputs[name])
        arrays[f"in_{name}_dram"] = a
        args.append(nc.dram_tensor(f"in_{name}_dram", a.shape, _mybir.dt.from_np(a.dtype), kind="ExternalInput").ap())
    shape = inputs["x"].shape
    o = nc.dram_tensor("out_0_dram", tuple(shape), _mybir.dt.float32, kind="ExternalOutput").ap()
    xattn_ffn_kernel(nc, *args, o)
    r = _run(nc, [arrays], core_ids=[0])
    return r.results[0]["out_0_dram"]
```

```python
from contextlib import ExitStack

import concourse.bass as bass
from concourse import mybir

F32 = mybir.dt.float32
BF16 = mybir.dt.bfloat16
F16 = mybir.dt.float16
I32 = mybir.dt.int32
U32 = mybir.dt.uint32
ALU = mybir.AluOpType
ACT = mybir.ActivationFunctionType
AX = mybir.AxisListType

P = 128
LN_EPS = 1e-5
ROUTED_SCALE = 2.5
W_SCALE = 256.0
G_SCALE = 16.0
QH = 32
TOP_K = 2


def xattn_ffn_kernel(nc, x, ctx_in, gate_w, w1, w2, w3, sw1, sw2, sw3, out):
    B, S, D = x.shape
    C = ctx_in.shape[2]
    E, _, H = w1.shape
    HD = D // QH
    KV = C // HD
    G = QH // KV
    ST = S // P
    N = B * S
    NT = N // P
    DC = D // P
    XC = D + C
    BLK = XC // P
    HC = -(-H // P)
    HL = H - (HC - 1) * P
    RT = (N * TOP_K) // P + E
    TILES = NT + RT
    SLOTS = TILES * P
    ROW = D + 4
    AHEAD = 5
    NPART = 3
    PAIRS = ((0, 0), (1, 0), (2, 0), (0, 1), (1, 1), (0, 2))
    NP = len(PAIRS)
    KR = HD * NP
    NSLOT = 4
    UN = KV
    STORES = 16 * 2 * NP
    LOADS = 16 * 3
    SCALE = float(HD) ** -0.5
    assert HD == 16 and ST == 4 and G == 4 and UN % NSLOT == 0 and KR == 96 and TILES % 4 == 0

    x_rows = x.rearrange("b s d -> (b s) d")
    ctx_rows = ctx_in.rearrange("b s d -> (b s) d")
    out_rows = out.rearrange("b s d -> (b s) d")

    q_d = nc.dram_tensor("q_scratch", (B, D * NP, S), BF16).ap()
    k_d = nc.dram_tensor("k_scratch", (B, C * NP, S), BF16).ap()
    attn_d = nc.dram_tensor("attn_scratch", ((B + 1) * S, D), F32).ap()
    sum_d = nc.dram_tensor("sum_scratch", (N + P, D), F32).ap()
    xs_d = nc.dram_tensor("slots_in_scratch", (SLOTS, ROW), F32).ap()

    with ExitStack() as whole:
        def sb(stack, name, shape, dt):
            return stack.enter_context(nc.sbuf_tensor(name, shape, dt))

        def pb(stack, name, shape, dt):
            return stack.enter_context(nc.psum_tensor(name, shape, dt))

        def sem(stack, name):
            return stack.enter_context(nc.semaphore(name))

        W13 = sb(whole, "W13", [P, E + 1, DC, 2, 2 * H], F16)
        W2 = sb(whole, "W2", [P, E + 1, HC, 2, D], F16)
        identf = sb(whole, "identf", [P, P], F32)

        with ExitStack() as st:
            identb = sb(st, "identb", [P, P], BF16)
            xin = sb(st, "xin", [P, ST, XC], F32)
            bst = sb(st, "bst", [P, ST, 6], F32)
            mv = sb(st, "mv", [P, ST, 2], F32)
            veps = sb(st, "veps", [P, ST], F32)
            sdev = sb(st, "sdev", [P, ST], F32)
            rstd = sb(st, "rstd", [P, ST], F32)
            part = sb(st, "part", [P, 2, NPART, XC], BF16)
            rest = sb(st, "rest", [P, 2, XC], F32)
            stage = sb(st, "stage", [P, NPART, BLK, S], BF16)
            psT = [pb(st, f"psT{i}", [P, BLK, P], BF16) for i in range(2 * NPART)]
            s_id = sem(st, "a_ident")
            s_xin = [sem(st, f"a_xin{i}") for i in range(ST)]
            s_bst, s_mv, s_veps, s_sdev, s_rstd = (sem(st, f"a_{n}") for n in ("bst", "mv", "veps", "sdev", "rstd"))
            s_xn = sem(st, "a_xn")
            s_rest = sem(st, "a_rest")
            s_part = [sem(st, f"a_part{i}") for i in range(NPART)]
            s_turned = [sem(st, f"a_turned{i}") for i in range(NPART)]
            s_evac = [sem(st, f"a_evac{i}") for i in range(NPART)]
            s_stored = sem(st, "a_stored")

            with nc.Block() as block:
                @block.sync
                def _(sp):
                    def load(b, t):
                        at = bass.ds(b * S + t * P, P)
                        sp.dma_start(xin[:, t, 0:D], x_rows[at, :]).then_inc(s_xin[t], 16)
                        sp.dma_start(xin[:, t, D:XC], ctx_rows[at, :]).then_inc(s_xin[t], 16)

                    sp.sem_inc(s_stored, 1)

                    def step(b, last):
                        if not last:
                            for t in range(ST):
                                sp.wait_ge(s_rest, ST * b + t + 1)
                                sp.wait_ge(s_part[0], ST * b + t + 1)
                                load(b + 1, t)
                        for a in range(NPART):
                            sp.wait_ge(s_evac[a], ST * b + ST + 2)
                            for j, (qa, ka) in enumerate(PAIRS):
                                if qa == a:
                                    dst = q_d[bass.ds(b, 1)].rearrange("o (k p j) s -> p (o k) j s", p=P, j=NP)[:, :, j]
                                    sp.dma_start(dst, stage[:, a, 0:DC]).then_inc(s_stored, 16)
                                if ka == a:
                                    dst = k_d[bass.ds(b, 1)].rearrange("o (p j) s -> p o j s", j=NP)[:, :, j]
                                    sp.dma_start(dst, stage[:, a, DC:BLK]).then_inc(s_stored, 16)

                    for t in range(ST):
                        load(0, t)
                    with sp.Fori(0, B - 1) as b:
                        step(b, False)
                    step(B - 1, True)
                    sp.wait_ge(s_stored, STORES * B + 1)

                @block.gpsimd
                def _(pool):
                    nc.gpsimd.memset(identb[:], 0.0).then_inc(s_id, 1)
                    nc.gpsimd.memset(identf[:], 0.0).then_inc(s_id, 1)
                    pool.wait_ge(s_id, 2)
                    for m in (identb, identf):
                        nc.gpsimd.affine_select(out=m[:], in_=m[:], compare_op=ALU.not_equal, fill=1.0, base=0,
                                                pattern=[[-1, P]], channel_multiplier=1).then_inc(s_id, 1)

                @block.vector
                def _(dve):
                    with dve.Fori(0, B) as b:
                        def aggregate(t):
                            nc.vector.bn_aggr(mv[:, t], bst[:, t]).then_inc(s_mv, 1)

                        for t in range(ST):
                            dve.wait_ge(s_xin[t], 32 * b + 32)
                            if t >= 1:
                                dve.wait_ge(s_bst, ST * b + t)
                            nc.vector.bn_stats(bst[:, t], xin[:, t, 0:D]).then_inc(s_bst, 1)
                            if t >= 1:
                                aggregate(t - 1)
                        dve.wait_ge(s_bst, ST * b + ST)
                        dve.wait_ge(s_mv, ST * b + ST - 1)
                        nc.vector.tensor_scalar_add(veps[:, 0:ST - 1], mv[:, 0:ST - 1, 1], LN_EPS).then_inc(s_veps, 1)
                        aggregate(ST - 1)
                        dve.wait_ge(s_mv, ST * b + ST)
                        nc.vector.tensor_scalar_add(veps[:, ST - 1:ST], mv[:, ST - 1:ST, 1], LN_EPS).then_inc(s_veps, 1)
                        dve.wait_ge(s_sdev, b + 1)
                        nc.vector.reciprocal(rstd[:], sdev[:]).then_inc(s_rstd, 1)
                        dve.wait_ge(s_rstd, b + 1)

                        def norm(t):
                            nc.vector.tensor_scalar(xin[:, t, 0:D], xin[:, t, 0:D], mv[:, t, 0:1], rstd[:, t:t + 1],
                                                    ALU.subtract, ALU.mult).then_inc(s_xn, 1)

                        def first_rest(t):
                            dve.wait_ge(s_part[0], ST * b + t + 1)
                            nc.vector.tensor_tensor(rest[:, t % 2], xin[:, t], part[:, t % 2, 0],
                                                    ALU.subtract).then_inc(s_rest, 1)

                        def third_part(t):
                            dve.wait_ge(s_part[1], ST * b + t + 1)
                            nc.vector.tensor_tensor(part[:, t % 2, 2], rest[:, t % 2], part[:, t % 2, 1],
                                                    ALU.subtract).then_inc(s_part[2], 1)

                        def evac(t):
                            dve.wait_ge(s_turned[1], ST * b + t + 3)
                            nc.vector.tensor_copy(stage[:, 1, :, t * P:(t + 1) * P], psT[NPART * (t % 2) + 1][:])\
                                .then_inc(s_evac[1], 1)

                        for t in range(ST + 2):
                            if t < ST:
                                norm(t)
                                first_rest(t)
                            if 0 <= t - 1 < ST:
                                third_part(t - 1)
                            if 0 <= t - 2 < ST:
                                if t == 2:
                                    dve.wait_ge(s_stored, STORES * b + 1)
                                evac(t - 2)

                @block.scalar
                def _(act):
                    with act.Fori(0, B) as b:
                        act.wait_ge(s_veps, 2 * b + 2)
                        nc.scalar.activation(sdev[:], veps[:], ACT.Sqrt).then_inc(s_sdev, 1)

                        def part0(t):
                            act.wait_ge(s_xn, ST * b + t + 1)
                            act.wait_ge(s_turned[0], ST * b + t + 1)
                            nc.scalar.activation(part[:, t % 2, 0], xin[:, t], ACT.Copy).then_inc(s_part[0], 1)

                        def part1(t):
                            act.wait_ge(s_rest, ST * b + t + 1)
                            nc.scalar.activation(part[:, t % 2, 1], rest[:, t % 2], ACT.Copy).then_inc(s_part[1], 1)

                        def evac(t, a):
                            act.wait_ge(s_turned[a], ST * b + t + 3)
                            nc.scalar.activation(stage[:, a, :, t * P:(t + 1) * P], psT[NPART * (t % 2) + a][:],
                                                 ACT.Copy).then_inc(s_evac[a], 1)

                        for t in range(ST + 1):
                            if t < ST:
                                part0(t)
                                part1(t)
                            if t >= 1:
                                if t == 1:
                                    act.wait_ge(s_stored, STORES * b + 1)
                                evac(t - 1, 0)
                                evac(t - 1, 2)

                @block.tensor
                def _(pe):
                    for a in range(NPART):
                        pe.sem_inc(s_turned[a], 2)
                        pe.sem_inc(s_evac[a], 2)
                    pe.wait_ge(s_id, 4)
                    with pe.Fori(0, B) as b:
                        for t in range(ST):
                            for a in range(NPART):
                                pe.wait_ge(s_part[a], ST * b + t + 1)
                                pe.wait_ge(s_evac[a], ST * b + t + 1)
                                for k in range(BLK):
                                    last = nc.tensor.transpose(psT[NPART * (t % 2) + a][:, k], part[:, t % 2, a, k * P:(k + 1) * P],
                                                               identb[:])
                                last.then_inc(s_turned[a], 1)

        with ExitStack() as st:
            qs = sb(st, "qs", [P, NSLOT, G, S], BF16)
            ks = sb(st, "ks", [P, NSLOT, S], BF16)
            va = sb(st, "va", [P, NSLOT, ST, 32], F32)
            pr = sb(st, "pr", [P, 2, G, S], F32)
            ot = sb(st, "ot", [P, S], F32)
            nmax = sb(st, "nmax", [P, 2, G * ST], F32)
            nrow = sb(st, "nrow", [G * ST, 2, P], BF16)
            rec = sb(st, "rec", [P, ST, G], F32)
            ob = sb(st, "ob", [P, 2, ST, G * HD], F32)
            wst = sb(st, "wst", [P, 2, DC * H], F32)
            w_scale = sb(st, "w_scale", [P, 1], F32)
            zrow = sb(st, "zrow", [P, ROW // 4], F32)
            psS = [pb(st, f"psS{i}", [P, S], F32) for i in range(2)]
            psM = pb(st, "psM", [P, 2, 2, S], F32)
            psO = pb(st, "psO", [P, S], F32)
            psX = pb(st, "psX", [P, ST, P], F32)

            s_init = sem(st, "b_init")
            s_load = [sem(st, f"b_load{i}") for i in range(NSLOT)]
            s_row = [sem(st, f"b_row{i}") for i in range(NSLOT)]
            s_store = [sem(st, f"b_store{i}") for i in range(2)]
            s_mscore, s_nmax, s_nmaxT, s_nrow = (sem(st, f"b_{n}") for n in ("mscore", "nmax", "nmaxT", "nrow"))
            s_score, s_exp, s_pv, s_ocopy, s_oT, s_rec, s_out = (
                sem(st, f"b_{n}") for n in ("score", "exp", "pv", "ocopy", "oT", "rec", "out"))
            s_w = [sem(st, f"b_w{i}") for i in range(2)]
            s_wsc, s_whi, s_wlo, s_zero, s_zd = (sem(st, f"b_{n}") for n in ("wsc", "whi", "wlo", "zero", "zd"))

            with nc.Block() as block:
                @block.sync
                def _(sp):
                    def load_unit(b, k):
                        n = k % NSLOT
                        b, k = b + k // UN, k % UN
                        src = q_d[bass.ds(b, 1), k * G * KR:(k + 1) * G * KR, :]
                        sp.dma_start(qs[0:KR, n], src.rearrange("o (g r) s -> r (o g) s", g=G)).then_inc(s_load[n], 16)
                        src = k_d[bass.ds(b, 1), k * KR:(k + 1) * KR, :]
                        sp.dma_start(ks[0:KR, n], src.rearrange("o r s -> r (o s)")).then_inc(s_load[n], 16)
                        src = ctx_rows[bass.ds(b * S, S), k * HD:(k + 1) * HD]
                        sp.dma_start(va[:, n, :, 0:HD], src.rearrange("(t p) d -> p t d", p=P)).then_inc(s_load[n], 16)

                    def send_row(b, k):
                        n = k % NSLOT
                        sp.wait_ge(s_nrow, UN * b + k + 1)
                        sp.dma_start(qs[KR:KR + 1, n].rearrange("o g s -> o (g s)"), nrow[:, k % 2]).then_inc(s_row[n], 16)

                    def store(b, k):
                        kk = (k - 1) % UN
                        row0 = (b + (1 if k else 0)) * S
                        sp.wait_ge(s_out, UN * b + k + 2)
                        dst = attn_d[bass.ds(row0, S), kk * G * HD:(kk + 1) * G * HD]
                        sp.dma_start(dst.rearrange("(t p) c -> p t c", p=P), ob[:, k % 2]).then_inc(s_store[k % 2], 16)

                    def batch(b, last):
                        for k in range(UN):
                            if not last or k + 1 < UN:
                                send_row(b, k + 1)
                            if not last or k + 3 < UN:
                                sp.wait_ge(s_pv, 4 * (UN * b + k) + 2)
                                load_unit(b, k + 3)
                            store(b, k)

                    for n in range(2):
                        sp.sem_inc(s_store[n], 1)
                    sp.wait_ge(s_init, 6)
                    for k in range(3):
                        load_unit(0, k)
                    send_row(0, 0)
                    with sp.Fori(0, B - 1) as b:
                        batch(b, False)
                    batch(B - 1, True)
                    store(B, 0)
                    sp.wait_ge(s_store[0], 16 * (UN * B // 2 + 1) + 1)
                    sp.wait_ge(s_store[1], 16 * (UN * B // 2) + 1)

                @block.tensor
                def _(pe):
                    def max_scores(b, k, j):
                        n, (t, g) = k % NSLOT, divmod(j, G)
                        u = UN * b + k
                        if j == 0:
                            pe.wait_ge(s_load[n], LOADS * (UN // NSLOT * b + k // NSLOT + 1))
                        if j % 2 == 0 and (k >= 1 or j >= 4):
                            pe.wait_ge(s_nmax, 8 * u + j // 2 - 1)
                        mm = nc.tensor.matmul(psM[:, j // 2 % 2, j % 2], qs[0:KR, n, g, t * P:(t + 1) * P], ks[0:KR, n],
                                              start=True, stop=True)
                        if j % 2:
                            mm.then_inc(s_mscore, 1)

                    def turn_max(b, k):
                        u = UN * b + k
                        pe.wait_ge(s_nmax, 8 * (u + 1))
                        if k >= 1:
                            pe.wait_ge(s_out, u)
                        nc.tensor.transpose(psX[0:G * ST, 0], nmax[:, k % 2], identf[:]).then_inc(s_nmaxT, 1)

                    def turn_out(b, k, row):
                        u = UN * b + k
                        pe.wait_ge(s_ocopy, u + 1)
                        if row:
                            pe.wait_ge(s_nrow, u + 2)
                        else:
                            pe.wait_ge(s_out, u + 1)
                        for t in range(ST):
                            last = nc.tensor.transpose(psX[:, t], ot[:, t * P:(t + 1) * P], identf[:])
                        last.then_inc(s_oT, 1)

                    def scores(b, k, t, g):
                        n = k % NSLOT
                        pe.wait_ge(s_exp, ST * G * (UN * b + k) + G * t + g + 1)
                        nc.tensor.matmul(psS[g % 2][:], ks[0:KR + 1, n, t * P:(t + 1) * P], qs[0:KR + 1, n, g],
                                         start=True, stop=True).then_inc(s_score, 1)

                    def values(n, t):
                        for g in range(G):
                            last = nc.tensor.matmul(psO[32 * g:32 * g + 32], va[:, n, t], pr[:, t % 2, g],
                                                    start=(t == 0), stop=(t == ST - 1))
                        last.then_inc(s_pv, 1)

                    def batch(b, last):
                        for k in range(UN):
                            n = k % NSLOT
                            pe.wait_ge(s_row[n], 16 * (UN // NSLOT * b + k // NSLOT + 1))
                            more = not last or k + 1 < UN
                            for t in range(ST):
                                scores(b, k, t, 0)
                                scores(b, k, t, 1)
                                pe.wait_ge(s_exp, ST * G * (UN * b + k) + G * t + 2)
                                if t == 0:
                                    values((k - 1) % NSLOT, ST - 1)
                                else:
                                    if t == 1:
                                        pe.wait_ge(s_ocopy, UN * b + k + 1)
                                    values(n, t - 1)
                                scores(b, k, t, 2)
                                scores(b, k, t, 3)
                                if not last or k + 2 < UN:
                                    for g in range(G):
                                        max_scores(b, k + 2, G * t + g)
                                if t == 0 and more:
                                    turn_max(b, k + 1)
                                if t == 2:
                                    turn_out(b, k, more)

                    pe.wait_ge(s_init, 6)
                    pe.sem_inc(s_oT, 1)
                    values(NSLOT - 1, 0)
                    for j in range(G * ST):
                        max_scores(0, 0, j)
                    turn_max(0, 0)
                    for j in range(G * ST):
                        max_scores(0, 1, j)
                    with pe.Fori(0, B - 1) as b:
                        batch(b, False)
                    batch(B - 1, True)
                    pe.wait_ge(s_exp, ST * G * UN * B + 2)
                    values((UN - 1) % NSLOT, ST - 1)
                    turn_out(B, 0, False)

                @block.vector
                def _(dve):
                    def maximum(b, k, i):
                        u = UN * b + k
                        t, g = i // 2, i % 2 * 2
                        if i == 0 and k >= 2:
                            dve.wait_ge(s_nmaxT, u - 1)
                        dve.wait_ge(s_mscore, 8 * u + i + 1)
                        to = nmax[:, k % 2].rearrange("p (g t) -> p g t", t=ST)[:, g:g + 2, t]
                        nc.vector.tensor_reduce(to, psM[:, i % 2], AX.X, ALU.max, negate=True).then_inc(s_nmax, 1)

                    def row(b, k):
                        u = UN * b + k
                        dve.wait_ge(s_nmaxT, u + 1)
                        if k >= 2:
                            m = k - 2
                            dve.wait_ge(s_row[m % NSLOT], 16 * (UN // NSLOT * b + m // NSLOT + 1))
                        nc.vector.tensor_copy(nrow[:, k % 2], psX[0:G * ST, 0]).then_inc(s_nrow, 1)

                    def normalise(b, k):
                        u = UN * b + k
                        dve.wait_ge(s_oT, u + 2)
                        o = psX[:].rearrange("p t (g c) -> p t g c", g=G)
                        nc.vector.reciprocal(rec[:], o[:, :, :, HD]).then_inc(s_rec, 1)
                        dve.wait_ge(s_rec, u + 1)
                        dve.wait_ge(s_store[k % 2], 16 * (UN // 2 * b + k // 2) + 1)
                        nc.vector.tensor_tensor(ob[:, k % 2].rearrange("p t (g d) -> p t g d", g=G), o[:, :, :, 0:HD],
                                                rec[:].unsqueeze(3).to_broadcast([P, ST, G, HD]),
                                                ALU.mult).then_inc(s_out, 1)

                    def batch(b, last):
                        for k in range(UN):
                            ahead = not last or k + 2 < UN
                            for i in range(8):
                                if ahead:
                                    maximum(b, k + 2, i)
                                if i == 1 and (not last or k + 1 < UN):
                                    row(b, k + 1)
                                if i == 5:
                                    normalise(b, k)

                    dve.sem_inc(s_out, 1)
                    nc.vector.memset(ks[KR:KR + 1], 1.0).then_inc(s_init, 1)
                    nc.vector.memset(va[:], 0.0).then_inc(s_init, 1)
                    nc.vector.memset(pr[:], 1.0).then_inc(s_init, 1)
                    dve.wait_ge(s_init, 3)
                    nc.vector.memset(va[:, :, :, HD:HD + 1], 1.0).then_inc(s_init, 3)
                    for i in range(8):
                        maximum(0, 0, i)
                    row(0, 0)
                    for i in range(8):
                        maximum(0, 1, i)
                    with dve.Fori(0, B - 1) as b:
                        batch(b, False)
                    batch(B - 1, True)
                    normalise(B, 0)

                @block.scalar
                def _(act):
                    def exps(b, k, t, g):
                        u = UN * b + k
                        act.wait_ge(s_score, ST * G * u + G * t + g + 1)
                        if g == 0:
                            act.wait_ge(s_pv, ST * u + t + 1)
                        nc.scalar.activation(pr[:, t % 2, g], psS[g % 2][:], ACT.Exp, scale=SCALE).then_inc(s_exp, 1)

                    def copy_out(b, k):
                        u = UN * b + k
                        act.wait_ge(s_pv, ST * u + 2)
                        act.wait_ge(s_oT, u + 1)
                        nc.scalar.activation(ot[:], psO[:], ACT.Copy).then_inc(s_ocopy, 1)

                    def batch(b):
                        for k in range(UN):
                            for t in range(ST):
                                for g in range(G):
                                    exps(b, k, t, g)
                                if t == 0:
                                    copy_out(b, k)

                    nc.scalar.activation(rec[:], identf[:, 0:ST * G].rearrange("p (t g) -> p t g", g=G), ACT.Copy).then_inc(s_exp, 2)
                    with act.Fori(0, B) as b:
                        batch(b)
                    copy_out(B, 0)

                @block.gpsimd
                def _(pool):
                    nc.gpsimd.memset(zrow[:], 0.0).then_inc(s_zero, 1)
                    nc.gpsimd.memset(wst[:], 0.0).then_inc(s_zero, 1)
                    nc.gpsimd.memset(w_scale[:], W_SCALE).then_inc(s_zero, 1)
                    pool.wait_ge(s_zero, 3)

                    def split(i, src, hi, lo):
                        c = w_scale[0:src.shape[0]]
                        if len(src.shape) == 3:
                            c = c.unsqueeze(2)
                        c = c.to_broadcast(list(src.shape))
                        nc.gpsimd.tensor_tensor(hi, src, c, ALU.mult).then_inc(s_whi, 1)
                        nc.gpsimd.tensor_tensor(src, src, c, ALU.mult).then_inc(s_wsc, 1)
                        pool.wait_ge(s_whi, i + 1)
                        pool.wait_ge(s_wsc, i + 1)
                        nc.gpsimd.tensor_tensor(lo, src, hi, ALU.subtract).then_inc(s_wlo, 1)

                    def expert(e, w1e, w3e, w2e, slot):
                        full = (HC - 1) * P
                        for half, w in enumerate((w1e, w3e)):
                            pool.wait_ge(s_zero, 3)
                            pool.wait_ge(s_wlo, 4 * e)
                            src = wst[:, half].rearrange("p (c h) -> p c h", h=H)
                            pool.dma_start(src, w.rearrange("(c p) h -> p c h", p=P)).then_inc(s_w[half], 16)
                        for half in range(2):
                            pool.wait_ge(s_w[half], 32 * e + 16)
                            dst = W13[:, slot, :, :, half * H:(half + 1) * H]
                            split(4 * e + half, wst[:, half].rearrange("p (c h) -> p c h", h=H),
                                  fold(dst[..., 0, :]), fold(dst[..., 1, :]))
                        pool.wait_ge(s_zero, 3)
                        pool.wait_ge(s_wlo, 4 * e + 2)
                        pool.dma_start(wst[:, 0, 0:(HC - 1) * D].rearrange("p (c d) -> p c d", d=D),
                                       w2e[0:full].rearrange("(c p) d -> p c d", p=P)).then_inc(s_w[0], 16)
                        pool.dma_start(wst[0:HL, 1, 0:D], w2e[full:H]).then_inc(s_w[1], 16)
                        pool.wait_ge(s_w[0], 32 * e + 32)
                        split(4 * e + 2, wst[:, 0, 0:(HC - 1) * D].rearrange("p (c d) -> p c d", d=D),
                              fold(W2[:, slot, 0:HC - 1, 0]), fold(W2[:, slot, 0:HC - 1, 1]))
                        pool.wait_ge(s_w[1], 32 * e + 32)
                        split(4 * e + 3, wst[0:HL, 1:2, 0:D], fold(W2[0:HL, slot, HC - 1:HC, 0]),
                              fold(W2[0:HL, slot, HC - 1:HC, 1]))

                    def fold(ap):
                        return ap.squeeze(1) if len(ap.shape) == 4 else ap

                    expert(0, sw1, sw3, sw2, E)
                    cq = ROW // 4
                    for c in range(4):
                        if c == 3:
                            pool.wait_ge(s_zd, 48)
                            nc.gpsimd.iota(zrow[:, D + 1 - 3 * cq:D + 2 - 3 * cq], [[0, 1]], base=N, channel_multiplier=1,
                                           allow_small_or_imprecise_dtypes=True).then_inc(s_zero, 1)
                            pool.wait_ge(s_zero, 4)
                        pool.dma_start(xs_d[N:SLOTS, c * cq:(c + 1) * cq].rearrange("(t p) c -> p t c", p=P),
                                       zrow[:].unsqueeze(1).to_broadcast([P, RT, cq])).then_inc(s_zd, 16)
                    with pool.Fori(0, E) as e:
                        one = bass.ds(e, 1)
                        expert(e + 1, w1[one].squeeze(0), w3[one].squeeze(0), w2[one].squeeze(0), one)
                    pool.wait_ge(s_wlo, 4 * (E + 1))
                    pool.wait_ge(s_zd, 64)

        with ExitStack() as st_cd:
            slot_i = sb(st_cd, "slot_i", [P, TOP_K, NT], I32)
            tile_w = sb(st_cd, "tile_w", [P, TILES // 4], I32)
            wts = sb(st_cd, "wts", [P, TOP_K, NT], F32)
            with ExitStack() as st:
                xin = sb(st, "xin2", [P, ST, D], F32)
                ain = sb(st, "ain", [P, ST, D], F32)
                xn = sb(st, "xn", [P, ST, ROW], F32)
                bst = sb(st, "bst2", [P, ST, 6], F32)
                mv = sb(st, "mv2", [P, ST, 2], F32)
                veps = sb(st, "veps2", [P, ST], F32)
                sdev = sb(st, "sdev2", [P, ST], F32)
                rstd = sb(st, "rstd2", [P, ST], F32)
                xT = sb(st, "xT", [P, 2, DC, P], F32)
                gw = sb(st, "gw", [E, D], F32)
                gwT = sb(st, "gwT", [P, DC, E], F32)
                lg = sb(st, "lg", [P, NT, E], F32)
                sc = sb(st, "sc", [P, NT, E], F32)
                mx = sb(st, "mx", [P, NT, 8], F32)
                ix = sb(st, "ix", [P, NT, 8], U32)
                ixf = sb(st, "ixf", [P, NT, TOP_K], F32)
                iota_e = sb(st, "iota_e", [P, NT, E], F32)
                iota_t = sb(st, "iota_t", [P, RT], F32)
                before = sb(st, "before", [P, P], F32)
                ones = sb(st, "ones", [P, P], F32)
                pick = sb(st, "pick", [P, TOP_K, NT, E], F32)
                both = sb(st, "both", [P, NT, E], F32)
                cum = sb(st, "cum", [P, NT + 1, E], F32)
                tot = sb(st, "tot", [P, NT, E], F32)
                cnt_i = sb(st, "cnt_i", [P, 3, E], I32)
                padf = sb(st, "padf", [P, E], F32)
                base = sb(st, "base", [P, E + 1], F32)
                slots = sb(st, "slots", [P, NT, E], F32)
                hit = sb(st, "hit", [P, NT, E], F32)
                slotf = sb(st, "slotf", [P, TOP_K, NT], F32)
                den = sb(st, "den", [P, 2, NT], F32)
                past = sb(st, "past", [P, RT, E], F32)
                tef = sb(st, "tef", [P, TILES + 8], F32)
                words = sb(st, "words", [P, TILES // 4], F32)
                psT = [pb(st, f"psT2{i}", [P, DC, P], F32) for i in range(2)]
                psL = [pb(st, f"psL{i}", [P, E], F32) for i in range(2)]
                psC = [pb(st, f"psC{i}", [P, NT, E], F32) for i in range(2)]
                psG = pb(st, "psG", [P, DC, E], F32)

                s_x = [sem(st, f"c_in{i}") for i in range(ST)]
                s_sum = [sem(st, f"c_sum{i}") for i in range(ST)]
                s_row = [sem(st, f"c_row{i}") for i in range(ST)]
                s_gw = sem(st, "c_gw")
                s_cst, s_gT, s_gwT, s_x1, s_bst, s_mv, s_veps, s_sdev, s_rstd, s_xn = (
                    sem(st, f"c_{n}") for n in ("cst", "gT", "gwT", "x1", "bst", "mv", "veps", "sdev", "rstd", "xn"))
                s_xTp, s_xT, s_log, s_lg, s_sc, s_both, s_count, s_v = (
                    sem(st, f"c_{n}") for n in ("xTp", "xT", "log", "lg", "sc", "both", "count", "v"))

                with nc.Block() as block:
                    @block.sync
                    def _(sp):
                        def load(b, t):
                            at = b * S + t * P
                            sp.dma_start(xin[:, t], x_rows[bass.ds(at, P), :]).then_inc(s_x[t], 16)
                            sp.dma_start(ain[:, t], attn_d[bass.ds(at + S, P), :]).then_inc(s_x[t], 16)

                        def step(b, last):
                            for t in range(ST):
                                sp.wait_ge(s_x1, ST * b + t + 1)
                                sp.dma_start(sum_d[bass.ds(b * S + t * P, P), :], xin[:, t]).then_inc(s_sum[t], 16)
                            for t in range(ST):
                                sp.wait_ge(s_xn, ST * b + t + 1)
                                sp.dma_start(xs_d[bass.ds(b * S + t * P, P), :], xn[:, t]).then_inc(s_row[t], 16)
                                if not last:
                                    sp.wait_ge(s_sum[t], 16 * b + 16)
                                    load(b + 1, t)

                        sp.dma_start(gw[:], gate_w).then_inc(s_gw, 16)
                        for t in range(ST):
                            sp.sem_inc(s_row[t], 1)
                            load(0, t)
                        with sp.Fori(0, B - 1) as b:
                            step(b, False)
                        step(B - 1, True)
                        for t in range(ST):
                            sp.wait_ge(s_sum[t], 16 * B)
                            sp.wait_ge(s_row[t], 16 * B + 1)

                    @block.gpsimd
                    def _(pool):
                        nc.gpsimd.iota(iota_e[:], [[0, NT], [1, E]], base=0, channel_multiplier=0,
                                       allow_small_or_imprecise_dtypes=True).then_inc(s_cst, 1)
                        nc.gpsimd.iota(iota_t[:], [[P, RT]], base=0, channel_multiplier=0,
                                       allow_small_or_imprecise_dtypes=True).then_inc(s_cst, 1)
                        nc.gpsimd.memset(ones[:], 1.0).then_inc(s_cst, 1)
                        pool.wait_ge(s_cst, 3)
                        nc.gpsimd.affine_select(out=before[:], in_=ones[:], compare_op=ALU.is_gt, fill=0.0, base=0,
                                                pattern=[[1, P]], channel_multiplier=-1).then_inc(s_cst, 1)
                        nc.gpsimd.memset(xn[:, :, D:ROW], 1.0 / (W_SCALE * G_SCALE)).then_inc(s_cst, 1)
                        pool.wait_ge(s_cst, 5)
                        nc.gpsimd.iota(xn[:, :, D + 1:D + 2], [[P, ST], [0, 1]], base=-S, channel_multiplier=1,
                                       allow_small_or_imprecise_dtypes=True).then_inc(s_cst, 1)
                    @block.scalar
                    def _(act):
                        act.sem_inc(s_xT, 2)
                        with act.Fori(0, B) as b:
                            act.wait_ge(s_veps, 2 * b + 2)
                            nc.scalar.activation(sdev[:], veps[:], ACT.Sqrt).then_inc(s_sdev, 1)
                            for t in range(ST):
                                act.wait_ge(s_xTp, ST * b + t + 1)
                                act.wait_ge(s_log, ST * b + t + 1)
                                nc.scalar.activation(xT[:, t % 2], psT[t % 2][:], ACT.Copy).then_inc(s_xT, 1)
                        act.wait_ge(s_lg, NT + 2)
                        nc.scalar.activation(sc[:], lg[:], ACT.Sigmoid).then_inc(s_sc, 1)

                    @block.tensor
                    def _(pe):
                        pe.wait_ge(s_gw, 16)
                        for c in range(DC):
                            last = nc.tensor.transpose(psG[:, c], gw[:, c * P:(c + 1) * P], identf[0:E, 0:E])
                        last.then_inc(s_gT, 1)
                        pe.wait_ge(s_gwT, 1)

                        pe.sem_inc(s_log, 2)

                        def turn(b, t):
                            pe.wait_ge(s_xn, ST * b + t + 1)
                            pe.wait_ge(s_xT, ST * b + t + 1)
                            for c in range(DC):
                                last = nc.tensor.transpose(psT[t % 2][:, c], xn[:, t, c * P:(c + 1) * P], identf[:])
                            last.then_inc(s_xTp, 1)

                        def logits(b, t):
                            pe.wait_ge(s_xT, ST * b + t + 3)
                            pe.wait_ge(s_lg, ST * b + t + 1)
                            for c in range(DC):
                                last = nc.tensor.matmul(psL[t % 2][:], xT[:, t % 2, c], gwT[:, c], start=(c == 0),
                                                        stop=(c == DC - 1))
                            last.then_inc(s_log, 1)

                        with pe.Fori(0, B) as b:
                            for t in range(ST):
                                turn(b, t)
                                if t:
                                    logits(b, t - 1)
                            logits(b, ST - 1)
                        pe.wait_ge(s_cst, 4)
                        pe.wait_ge(s_both, 1)
                        nc.tensor.matmul(psC[0][:].rearrange("p t e -> p (t e)"), before[:],
                                         both[:].rearrange("p t e -> p (t e)"), start=True, stop=True)
                        nc.tensor.matmul(psC[1][:].rearrange("p t e -> p (t e)"), ones[:],
                                         both[:].rearrange("p t e -> p (t e)"), start=True, stop=True).then_inc(s_count, 1)

                    @block.vector
                    def _(dve):
                        steps = [0]

                        def then(ins):
                            steps[0] += 1
                            ins.then_inc(s_v, 1)
                            dve.wait_ge(s_v, steps[0])

                        dve.wait_ge(s_gT, 1)
                        nc.vector.tensor_copy(gwT[:], psG[:]).then_inc(s_gwT, 1)
                        dve.sem_inc(s_lg, 2)
                        dve.wait_ge(s_cst, 6)

                        def norm(b, t):
                            dve.wait_ge(s_row[t], 16 * b + 1)
                            nc.vector.tensor_scalar(xn[:, t, 0:D], xin[:, t], mv[:, t, 0:1], rstd[:, t:t + 1],
                                                    ALU.subtract, ALU.mult)
                            nc.vector.tensor_scalar_add(xn[:, t, D + 1:D + 2], xn[:, t, D + 1:D + 2], float(S)).then_inc(s_xn, 1)

                        def take_logits(b, t):
                            dve.wait_ge(s_log, ST * b + t + 3)
                            nc.vector.tensor_copy(lg[:, bass.ds(ST * b + t, 1), :].rearrange("p o e -> p (o e)"), psL[t % 2][:])\
                                .then_inc(s_lg, 1)

                        with dve.Fori(0, B) as b:
                            for t in range(ST):
                                dve.wait_ge(s_x[t], 32 * b + 32)
                                if t >= 1:
                                    dve.wait_ge(s_bst, ST * b + t)
                                nc.vector.tensor_tensor(xin[:, t], xin[:, t], ain[:, t], ALU.add).then_inc(s_x1, 1)
                                if t >= 1:
                                    nc.vector.bn_aggr(mv[:, t - 1], bst[:, t - 1]).then_inc(s_mv, 1)
                                dve.wait_ge(s_x1, ST * b + t + 1)
                                nc.vector.bn_stats(bst[:, t], xin[:, t]).then_inc(s_bst, 1)
                            dve.wait_ge(s_bst, ST * b + ST)
                            dve.wait_ge(s_mv, ST * b + ST - 1)
                            nc.vector.tensor_scalar_add(veps[:, 0:ST - 1], mv[:, 0:ST - 1, 1], LN_EPS).then_inc(s_veps, 1)
                            nc.vector.bn_aggr(mv[:, ST - 1], bst[:, ST - 1]).then_inc(s_mv, 1)
                            dve.wait_ge(s_mv, ST * b + ST)
                            nc.vector.tensor_scalar_add(veps[:, ST - 1:ST], mv[:, ST - 1:ST, 1], LN_EPS).then_inc(s_veps, 1)
                            dve.wait_ge(s_sdev, b + 1)
                            nc.vector.reciprocal(rstd[:], sdev[:]).then_inc(s_rstd, 1)
                            dve.wait_ge(s_rstd, b + 1)
                            for t in range(ST + 1):
                                if t < ST:
                                    norm(b, t)
                                if t:
                                    take_logits(b, t - 1)
                        dve.wait_ge(s_sc, 1)
                        for t in range(NT):
                            last = nc.vector.max(mx[:, t], sc[:, t])
                        then(last)
                        for t in range(NT):
                            last = nc.vector.max_index(ix[:, t], mx[:, t], sc[:, t])
                        then(last)
                        then(nc.vector.tensor_copy(ixf[:], ix[:, :, 0:TOP_K]))
                        dve.wait_ge(s_cst, 4)
                        for k in range(TOP_K):
                            then(nc.vector.tensor_tensor(pick[:, k], iota_e[:], ixf[:, :, k:k + 1].to_broadcast([P, NT, E]),
                                                         ALU.is_equal))
                        nc.vector.tensor_tensor(both[:], pick[:, 0], pick[:, 1], ALU.add).then_inc(s_both, 1)
                        then(nc.vector.tensor_tensor(den[:, 0], mx[:, :, 0], mx[:, :, 1], ALU.add))
                        then(nc.vector.tensor_scalar_add(den[:, 0], den[:, 0], 1e-20))
                        then(nc.vector.reciprocal(den[:, 1], den[:, 0]))
                        for k in range(TOP_K):
                            then(nc.vector.tensor_tensor(wts[:, k], mx[:, :, k], den[:, 1], ALU.mult))
                        then(nc.vector.tensor_scalar_mul(wts[:], wts[:], ROUTED_SCALE / (W_SCALE * G_SCALE)))
                        dve.wait_ge(s_count, 1)
                        then(nc.vector.tensor_copy(tot[:], psC[1][:]))
                        then(nc.vector.memset(cum[:, 0], 0.0))
                        for t in range(NT):
                            then(nc.vector.tensor_tensor(cum[:, t + 1], cum[:, t], tot[:, t], ALU.add))
                        then(nc.vector.tensor_scalar_add(padf[:], cum[:, NT], float(P - 1)))
                        then(nc.vector.tensor_copy(cnt_i[:, 0], padf[:]))
                        then(nc.vector.tensor_single_scalar(cnt_i[:, 1], cnt_i[:, 0], P.bit_length() - 1, ALU.arith_shift_right))
                        then(nc.vector.tensor_copy(padf[:], cnt_i[:, 1]))
                        then(nc.vector.tensor_scalar_mul(padf[:], padf[:], float(P)))
                        then(nc.vector.memset(base[:, 0:1], 0.0))
                        for e in range(E):
                            then(nc.vector.tensor_tensor(base[:, e + 1:e + 2], base[:, e:e + 1], padf[:, e:e + 1], ALU.add))
                        then(nc.vector.tensor_tensor(slots[:], cum[:, 0:NT], psC[0][:], ALU.add))
                        then(nc.vector.tensor_tensor(slots[:], slots[:], base[:, 0:E].unsqueeze(1).to_broadcast([P, NT, E]), ALU.add))
                        for k in range(TOP_K):
                            then(nc.vector.tensor_tensor(hit[:], slots[:], pick[:, k], ALU.mult))
                            then(nc.vector.tensor_reduce(slotf[:, k], hit[:], AX.X, ALU.add))
                        then(nc.vector.tensor_scalar_add(slotf[:], slotf[:], float(N)))
                        then(nc.vector.tensor_copy(slot_i[:], slotf[:]))
                        then(nc.vector.tensor_tensor(past[:], iota_t[:].unsqueeze(2).to_broadcast([P, RT, E]),
                                                     base[:, 1:E + 1].unsqueeze(1).to_broadcast([P, RT, E]), ALU.is_ge))
                        then(nc.vector.memset(tef[:], float(E)))
                        then(nc.vector.tensor_reduce(tef[:, NT:TILES], past[:], AX.X, ALU.add))
                        then(nc.vector.tensor_scalar_min(tef[:, NT:TILES], tef[:, NT:TILES], float(E - 1)))
                        then(nc.vector.tensor_copy(words[:], tef[:, 2:TILES + 2:4]))
                        for n in range(1, AHEAD):
                            then(nc.vector.scalar_tensor_tensor(words[:], tef[:, 2 + n:TILES + 2 + n:4], 16.0 ** n, words[:],
                                                                ALU.mult, ALU.add))
                        nc.vector.tensor_copy(tile_w[:], words[:])

            with ExitStack() as st:
                xr = sb(st, "xr", [P, NT, ROW], F32)
                xt = sb(st, "xt", [P, 2, ROW], F32)
                xh = sb(st, "xh", [P, 2, DC, P], F16)
                xl = sb(st, "xl", [P, 2, DC, P], F16)
                sg = sb(st, "sg", [P, 2, H], F32)
                gg = sb(st, "gg", [P, 2, HC * P], F32)
                gh = sb(st, "gh", [P, 2, HC, P], F16)
                gl = sb(st, "gl", [P, 2, HC, P], F16)
                yo = sb(st, "yo", [P, 2, D], F32)
                wtc = sb(st, "wtc", [P, 2, 1], F32)
                num = sb(st, "num", [P, 2, 1], I32)
                psXT = pb(st, "psXT", [P, DC, P], F32)
                psH = pb(st, "psH", [P, 512], F32)
                psU = pb(st, "psU", [P, 512], F32)
                psGT = pb(st, "psGT", [P, HC, P], F32)
                psY = [pb(st, f"psY{i}", [P, D], F32) for i in range(2)]
                s_init = sem(st, "d_init")
                s_xr, s_xrn, s_xrw, s_sent, s_added, s_num, s_done = (
                    sem(st, f"d_{n}") for n in ("xr", "xrn", "xrw", "sent", "added", "num", "done"))
                s_xt = [sem(st, f"d_xt{i}") for i in range(2)]
                s_xT, s_xh, s_xl, s_hu, s_sg, s_g, s_gT, s_gh, s_gl, s_y, s_yo, s_wt = (
                    sem(st, f"d_{n}") for n in ("xT", "xh", "xl", "hu", "sg", "g", "gT", "gh", "gl", "y", "yo", "wt"))

                with nc.Block() as block:
                    @block.sync
                    def _(sp):
                        def load(i, j):
                            sp.dma_start(xt[:, j], xs_d[bass.ds(i * P, P), :]).then_inc(s_xt[j], 16)

                        def next_load(i, j):
                            sp.wait_ge(s_xT, i + 1)
                            sp.wait_ge(s_wt, i + 1)
                            sp.wait_ge(s_num, i + 1)
                            load(i + 2, j)

                        load(0, 0)
                        load(1, 1)
                        sp.dma_start(xr[:], xs_d[0:N].rearrange("(t p) c -> p t c", p=P)).then_inc(s_xr, 16)
                        with sp.Fori(0, NT // 2 - 1) as m:
                            for j in range(2):
                                next_load(2 * m + j, j)
                        sp.wait_ge(s_sent, 16 * NT * TOP_K)
                        with sp.Fori(NT // 2 - 1, TILES // 2 - 1) as m:
                            for j in range(2):
                                next_load(2 * m + j, j)
                        sp.wait_ge(s_added, 16 * TILES)
                        sp.dma_start(out_rows, sum_d[0:N]).then_inc(s_done, 16)
                        sp.wait_ge(s_done, 16)

                    @block.gpsimd
                    def _(pool):
                        def add(i):
                            pool.wait_ge(s_yo, i + 1)
                            pool.wait_ge(s_num, i + 1)
                            if i:
                                pool.wait_ge(s_added, 16 * i)
                            nc.gpsimd.indirect_dma_start(
                                out=sum_d, out_offset=bass.IndirectOffsetOnAxis(ap=num[:, i % 2].bitcast(U32), axis=0),
                                in_=yo[:, i % 2], in_offset=None, compute_op=ALU.add).then_inc(s_added, 16)

                        pool.wait_ge(s_xr, 16)
                        added = 0
                        for k in range(TOP_K):
                            if k:
                                pool.wait_ge(s_sent, 16 * NT * k)
                            nc.gpsimd.tensor_copy(xr[:, :, D:D + 1], wts[:, k].unsqueeze(2)).then_inc(s_xrw, 1)
                            if not k:
                                nc.gpsimd.iota(xr[:, :, D + 1:D + 2], [[P, NT], [0, 1]], base=0, channel_multiplier=1,
                                               allow_small_or_imprecise_dtypes=True).then_inc(s_xrn, 1)
                                pool.wait_ge(s_xrn, 1)
                            pool.wait_ge(s_xrw, k + 1)
                            for t in range(NT):
                                nc.gpsimd.indirect_dma_start(
                                    out=xs_d, out_offset=bass.IndirectOffsetOnAxis(ap=slot_i[:, k, t:t + 1].bitcast(U32), axis=0),
                                    in_=xr[:, t], in_offset=None).then_inc(s_sent, 16)
                                if t % 4 == 3:
                                    add(added)
                                    added += 1
                        for i in range(added, TILES):
                            add(i)
                        pool.wait_ge(s_added, 16 * TILES)

                    @block.tensor
                    def _(pe):
                        def experts_of(m, count):
                            word = pe.value_load(tile_w[0:1, bass.ds(m, 1)], min_val=0, max_val=16 ** AHEAD - 1)
                            return [pe.snap(((word >> (4 * n)) & 15).with_bounds(min_val=0, max_val=E)) for n in range(count)]

                        def turn_x(i, j, half):
                            pe.wait_ge(s_xt[j], 16 * half + 16)
                            pe.wait_ge(s_xh, i)
                            pe.wait_ge(s_xl, i)
                            for c in range(DC):
                                last = nc.tensor.transpose(psXT[:, c], xt[:, j, c * P:(c + 1) * P], identf[:])
                            last.then_inc(s_xT, 1)

                        def up(i, j, e):
                            pe.wait_ge(s_xh, i + 1)
                            pe.wait_ge(s_xl, i + 1)
                            pe.wait_ge(s_g, i)
                            n = 0
                            for c in range(DC):
                                for xp, wp in ((xh, 0), (xh, 1), (xl, 0)):
                                    for ps, at in ((psH, 0), (psU, H)):
                                        last = nc.tensor.matmul(
                                            ps[:, 0:H], xp[:, j, c],
                                            W13[:, bass.ds(e, 1), c, wp, at:at + H].rearrange("p o h -> p (o h)"),
                                            start=(n == 0), stop=(n == 3 * DC - 1))
                                    n += 1
                            last.then_inc(s_hu, 1)

                        def turn_g(i, j):
                            pe.wait_ge(s_g, i + 1)
                            pe.wait_ge(s_gh, i)
                            pe.wait_ge(s_gl, i)
                            for c in range(HC):
                                last = nc.tensor.transpose(psGT[:, c], gg[:, j, c * P:(c + 1) * P], identf[:])
                            last.then_inc(s_gT, 1)

                        def down(i, j, e):
                            pe.wait_ge(s_gh, i + 1)
                            pe.wait_ge(s_gl, i + 1)
                            if not isinstance(i, int) or i >= 2:
                                pe.wait_ge(s_yo, i - 1)
                            n = 0
                            for c in range(HC):
                                rows = P if c < HC - 1 else HL
                                for gp, wp in ((gh, 0), (gh, 1), (gl, 0)):
                                    last = nc.tensor.matmul(
                                        psY[j][:], gp[0:rows, j, c],
                                        W2[0:rows, bass.ds(e, 1), c, wp, :].rearrange("p o d -> p (o d)"),
                                        start=(n == 0), stop=(n == 3 * HC - 1))
                                    n += 1
                            last.then_inc(s_y, 1)

                        turn_x(0, 0, 0)
                        up(0, 0, E)
                        turn_x(1, 1, 0)
                        turn_g(0, 0)
                        up(1, 1, E)
                        turn_x(2, 0, 1)
                        down(0, 0, E)
                        turn_g(1, 1)
                        up(2, 0, E)
                        turn_x(3, 1, 1)
                        down(1, 1, E)
                        turn_g(2, 0)
                        with pe.Fori(0, TILES // 4 - 1) as m:
                            e = experts_of(m, AHEAD)
                            for n in range(2, AHEAD + 1):
                                i = 4 * m + n
                                up(i + 1, (n + 1) % 2, e[n - 1])
                                turn_x(i + 2, n % 2, 2 * m + (n + 2) // 2)
                                down(i, n % 2, e[n - 2])
                                turn_g(i + 1, (n + 1) % 2)
                        e = experts_of(TILES // 4 - 1, 2)
                        up(TILES - 1, 1, e[1])
                        down(TILES - 2, 0, e[0])
                        turn_g(TILES - 1, 1)
                        down(TILES - 1, 1, e[1])

                    @block.scalar
                    def _(act):
                        def split_x(i, j):
                            act.wait_ge(s_xT, i + 1)
                            if not isinstance(i, int) or i >= 2:
                                act.wait_ge(s_hu, i - 1)
                            nc.scalar.activation(xh[:, j], psXT[:], ACT.Copy).then_inc(s_xh, 1)

                        def silu(i, j):
                            act.wait_ge(s_hu, i + 1)
                            nc.scalar.activation(sg[:, j], psH[:, 0:H], ACT.Silu, scale=1.0 / W_SCALE).then_inc(s_sg, 1)

                        def split_g(i, j):
                            act.wait_ge(s_gT, i + 1)
                            if not isinstance(i, int) or i >= 2:
                                act.wait_ge(s_y, i - 1)
                            nc.scalar.activation(gh[:, j], psGT[:], ACT.Copy).then_inc(s_gh, 1)

                        def result(i, j):
                            act.wait_ge(s_y, i + 1)
                            act.wait_ge(s_wt, i + 1)
                            if not isinstance(i, int) or i >= 2:
                                act.wait_ge(s_added, 16 * (i - 1))
                            nc.scalar.activation(yo[:, j], psY[j][:], ACT.Copy, scale=wtc[:, j]).then_inc(s_yo, 1)

                        def tile(i, j, first=False, last=False):
                            silu(i, j)
                            if not last:
                                split_x(i + 1, 1 - j)
                            if not first:
                                result(i - 1, 1 - j)
                            split_g(i, j)

                        split_x(0, 0)
                        tile(0, 0, first=True)
                        tile(1, 1)
                        tile(2, 0)
                        tile(3, 1)
                        with act.Fori(2, TILES // 2 - 1) as m:
                            tile(2 * m, 0)
                            tile(2 * m + 1, 1)
                        tile(TILES - 2, 0)
                        tile(TILES - 1, 1, last=True)
                        result(TILES - 1, 1)

                    @block.vector
                    def _(dve):
                        def split_x(i, j):
                            dve.wait_ge(s_xh, i + 1)
                            nc.vector.tensor_tensor(xl[:, j], psXT[:], xh[:, j], ALU.subtract).then_inc(s_xl, 1)

                        def gate(i, j):
                            dve.wait_ge(s_sg, i + 1)
                            if not isinstance(i, int) or i >= 2:
                                dve.wait_ge(s_gT, i - 1)
                            nc.vector.scalar_tensor_tensor(gg[:, j, 0:H], psU[:, 0:H], G_SCALE / W_SCALE, sg[:, j],
                                                           ALU.mult, ALU.mult).then_inc(s_g, 1)

                        def split_g(i, j):
                            dve.wait_ge(s_gh, i + 1)
                            nc.vector.tensor_tensor(gl[:, j], psGT[:], gh[:, j], ALU.subtract).then_inc(s_gl, 1)

                        def take_row_end(i, j, half):
                            dve.wait_ge(s_xt[j], 16 * half + 16)
                            if not isinstance(i, int) or i >= 2:
                                dve.wait_ge(s_yo, i - 1)
                            nc.vector.tensor_copy(wtc[:, j], xt[:, j, D:D + 1]).then_inc(s_wt, 1)
                            if not isinstance(i, int) or i >= 2:
                                dve.wait_ge(s_added, 16 * (i - 1))
                            nc.vector.tensor_copy(num[:, j], xt[:, j, D + 1:D + 2]).then_inc(s_num, 1)

                        def tile(i, j, half, last=False):
                            gate(i, j)
                            if not last:
                                split_x(i + 1, 1 - j)
                            split_g(i, j)
                            if not last:
                                take_row_end(i + 1, 1 - j, half + 1 if j else half)

                        nc.vector.memset(gg[:], 0.0).then_inc(s_init, 1)
                        dve.wait_ge(s_init, 1)
                        split_x(0, 0)
                        take_row_end(0, 0, 0)
                        tile(0, 0, 0)
                        tile(1, 1, 0)
                        with dve.Fori(1, TILES // 2 - 1) as m:
                            tile(2 * m, 0, m)
                            tile(2 * m + 1, 1, m)
                        tile(TILES - 2, 0, TILES // 2 - 1)
                        tile(TILES - 1, 1, TILES // 2 - 1, last=True)


_INS = ["x", "ctx_512", "L0_ffn_gate_w", "L0_ffn_w1", "L0_ffn_w2", "L0_ffn_w3", "L0_ffn_sw1", "L0_ffn_sw2", "L0_ffn_sw3"]


def kernel(**inputs):
    import numpy as _np
    import concourse.bacc as _bacc
    from concourse import mybir as _mybir
    from concourse.bass_utils import run_bass_kernel_spmd as _run

    nc = _bacc.Bacc("TRN2", target_bir_lowering=False, num_devices=1)
    arrays, args = {}, []
    for name in _INS:
        a = _np.ascontiguousarray(inputs[name])
        arrays[f"in_{name}_dram"] = a
        args.append(nc.dram_tensor(f"in_{name}_dram", a.shape, _mybir.dt.from_np(a.dtype), kind="ExternalInput").ap())
    shape = inputs["x"].shape
    o = nc.dram_tensor("out_0_dram", tuple(shape), _mybir.dt.float32, kind="ExternalOutput").ap()
    xattn_ffn_kernel(nc, *args, o)
    r = _run(nc, [arrays], core_ids=[0])
    return r.results[0]["out_0_dram"]
```

```python
from contextlib import ExitStack

import concourse.bass as bass
from concourse import mybir

F32 = mybir.dt.float32
BF16 = mybir.dt.bfloat16
F16 = mybir.dt.float16
I32 = mybir.dt.int32
U32 = mybir.dt.uint32
ALU = mybir.AluOpType
ACT = mybir.ActivationFunctionType
AX = mybir.AxisListType

P = 128
LN_EPS = 1e-5
ROUTED_SCALE = 2.5
W_SCALE = 256.0
G_SCALE = 16.0
QH = 32
TOP_K = 2


def xattn_ffn_kernel(nc, x, ctx_in, gate_w, w1, w2, w3, sw1, sw2, sw3, out):
    B, S, D = x.shape
    C = ctx_in.shape[2]
    E, _, H = w1.shape
    HD = D // QH
    KV = C // HD
    G = QH // KV
    ST = S // P
    N = B * S
    NT = N // P
    DC = D // P
    XC = D + C
    BLK = XC // P
    HC = -(-H // P)
    HL = H - (HC - 1) * P
    RT = (N * TOP_K) // P + E - 1
    TILES = NT + RT
    LAST = 3
    FIRST = NT - LAST
    WORDS = -(-TILES // 4)
    SHARE = -(-RT // E)
    SLOTS = (NT + E * SHARE) * P
    ROW = D + 4
    AHEAD = 5
    NPART = 3
    PAIRS = ((0, 0), (1, 0), (2, 0), (0, 1), (1, 1), (0, 2))
    NP = len(PAIRS)
    KR = HD * NP
    NSLOT = 4
    UN = KV
    STORES = 16 * 2 * NPART
    LOADS = 16 * (NPART + 2)
    SCALE = float(HD) ** -0.5
    assert HD == 16 and ST == 4 and G == 4 and UN % NSLOT == 0 and KR == 96 and TILES % 4 == 3 and N * TOP_K % P == 0

    x_rows = x.rearrange("b s d -> (b s) d")
    ctx_rows = ctx_in.rearrange("b s d -> (b s) d")
    out_rows = out.rearrange("b s d -> (b s) d")

    q_d = nc.dram_tensor("q_scratch", (B, DC, NPART, P, S), BF16).ap()
    k_d = nc.dram_tensor("k_scratch", (B, NP, C, S), BF16).ap()
    sum_d = nc.dram_tensor("sum_scratch", (S + N + P, D), F32).ap()
    xs_d = nc.dram_tensor("slots_in_scratch", (SLOTS, ROW), F32).ap()

    with ExitStack() as whole:
        def sb(stack, name, shape, dt):
            return stack.enter_context(nc.sbuf_tensor(name, shape, dt))

        def pb(stack, name, shape, dt):
            return stack.enter_context(nc.psum_tensor(name, shape, dt))

        def sem(stack, name):
            return stack.enter_context(nc.semaphore(name))

        identf = sb(whole, "identf", [P, P], F32)
        s_store = [sem(whole, f"b_store{i}") for i in range(2)]
        s_stored_last = sem(whole, "a_stored_last")

        with ExitStack() as st:
            identb = sb(st, "identb", [P, P], BF16)
            xin = sb(st, "xin", [P, NT, D], F32)
            xc = sb(st, "xc", [P, NT, XC], F32)
            bst = sb(st, "bst", [P, ST, 6], F32)
            mv = sb(st, "mv", [P, ST, 2], F32)
            eps = sb(st, "eps", [P, 1], F32)
            warm = sb(st, "warm", [P, 1], F32)
            sdev = sb(st, "sdev", [P, ST], F32)
            rstd = sb(st, "rstd", [P, ST], F32)
            part = sb(st, "part", [P, 2, NPART, XC], BF16)
            rest = sb(st, "rest", [P, 2, XC], F32)
            stage = sb(st, "stage", [P, B, NPART, BLK, S], BF16)
            psT = pb(st, "psT", [P, 2, NPART, 8, P], BF16)
            BANK = (0, 2, 1)
            s_id = sem(st, "a_ident")
            s_first = [sem(st, f"a_first{i}") for i in range(ST)]
            s_xin = sem(st, "a_xin")
            s_bst, s_mv, s_sdev, s_rstd = (sem(st, f"a_{n}") for n in ("bst", "mv", "sdev", "rstd"))
            s_xn = sem(st, "a_xn")
            s_rest = sem(st, "a_rest")
            s_part = [sem(st, f"a_part{i}") for i in range(NPART)]
            s_turned = [sem(st, f"a_turned{i}") for i in range(NPART)]
            s_evac = [sem(st, f"a_evac{i}") for i in range(2)]
            s_evac.append(s_evac[0])
            s_stored = sem(st, "a_stored")

            def step_of(b, t):
                return b + t // ST, t % ST, ST * b + t + 1

            def tile_at(ap, b, t):
                return ap[:, bass.ds(ST * b + t, 1)].rearrange("p o d -> p (o d)")

            def stage_at(b, t, parts):
                return stage[:, bass.ds(b, 1), parts, :, t * P:(t + 1) * P].rearrange("p o a k s -> p (o a) k s")

            with nc.Block() as block:
                @block.sync
                def _(sp):
                    for t in range(ST):
                        sp.dma_start(xin[:, t], x_rows[t * P:(t + 1) * P]).then_inc(s_first[t], 16)
                        sp.dma_start(xc[:, t, D:XC], ctx_rows[t * P:(t + 1) * P]).then_inc(s_first[t], 16)

                    def store_part(b, a, done):
                        sp.wait_ge(s_evac[a], ST * b + ST + 2)
                        dst = q_d[bass.ds(b, 1), :, a].rearrange("o c p s -> p (o c) s")
                        sp.dma_start(dst, stage[:, bass.ds(b, 1), a, 0:DC].rearrange("p o c s -> p (o c) s"))\
                            .then_inc(done, 16)
                        js = [j for j, (_, ka) in enumerate(PAIRS) if ka == a]
                        dst = k_d[bass.ds(b, 1), js[0]:js[-1] + 1].rearrange("o j p s -> p (o j) s")
                        src = stage[:, bass.ds(b, 1), a, DC].rearrange("p o s -> p (o s)")
                        sp.dma_start(dst, src.unsqueeze(1).to_broadcast([P, len(js), S])).then_inc(done, 16)

                    with sp.Fori(0, B - 1) as b:
                        for a in (1, 0, 2):
                            store_part(b, a, s_stored)
                    for a in (1, 0, 2):
                        store_part(B - 1, a, s_stored_last)
                    sp.wait_ge(s_stored, STORES * (B - 1))

                @block.gpsimd
                def _(pool):
                    def load(b):
                        at = bass.ds(b * S, S)
                        pool.dma_start(xin[:, bass.ds(ST * b, ST)], x_rows[at].rearrange("(t p) d -> p t d", p=P)).then_inc(s_xin, 16)
                        pool.dma_start(xc[:, bass.ds(ST * b, ST), D:XC], ctx_rows[at].rearrange("(t p) d -> p t d", p=P))\
                            .then_inc(s_xin, 16)

                    nc.gpsimd.memset(eps[:], LN_EPS).then_inc(s_id, 1)
                    pool.wait_ge(s_id, 1)
                    nc.gpsimd.memset(identb[:], 0.0).then_inc(s_id, 1)
                    pool.wait_ge(s_id, 2)
                    nc.gpsimd.affine_select(out=identb[:], in_=identb[:], compare_op=ALU.not_equal, fill=1.0, base=0,
                                            pattern=[[-1, P]], channel_multiplier=1).then_inc(s_id, 1)
                    load(1)
                    pool.wait_ge(s_id, 3)
                    nc.gpsimd.memset(identf[:], 0.0).then_inc(s_id, 1)
                    pool.wait_ge(s_id, 4)
                    nc.gpsimd.affine_select(out=identf[:], in_=identf[:], compare_op=ALU.not_equal, fill=1.0, base=0,
                                            pattern=[[-1, P]], channel_multiplier=1).then_inc(s_id, 1)

                    def step(b, ahead):
                        for t in range(ST):
                            if ahead and t == 1:
                                pool.wait_ge(s_xin, 32 * b + 32)
                                load(b + 2)
                            pool.wait_ge(s_part[1], ST * b + t + 1)
                            pool.wait_ge(s_turned[2], ST * b + t + 1)
                            nc.gpsimd.tensor_tensor(part[:, t % 2, 2], rest[:, t % 2], part[:, t % 2, 1],
                                                    ALU.subtract).then_inc(s_part[2], 1)

                    with pool.Fori(0, B - 2) as b:
                        step(b, True)
                    with pool.Fori(B - 2, B) as b:
                        step(b, False)

                @block.vector
                def _(dve):
                    def stats(b, t, first=False):
                        b, t, _ = step_of(b, t)
                        if first:
                            dve.wait_ge(s_first[t], 32)
                        else:
                            dve.wait_ge(s_xin, 32 * b)
                        nc.vector.bn_stats(bst[:, t], tile_at(xin, b, t)).then_inc(s_bst, 1)

                    def aggregate(t):
                        nc.vector.bn_aggr(mv[:, t % ST], bst[:, t % ST]).then_inc(s_mv, 1)

                    def norm(b, t, ahead):
                        b, t, n = step_of(b, t)
                        dve.wait_ge(s_sdev, n)
                        if ahead:
                            dve.wait_ge(s_bst, n + 1)
                        nc.vector.reciprocal(rstd[:, t:t + 1], sdev[:, t:t + 1]).then_inc(s_rstd, 1)
                        if ahead:
                            aggregate(t + 1)
                        dve.wait_ge(s_rstd, n)
                        src = tile_at(xin, b, t).rearrange("p (u g f) -> p u f g", g=G, f=HD)
                        dst = tile_at(xc, b, t)[:, 0:D].rearrange("p (u f g) -> p u f g", g=G, f=HD)
                        nc.vector.tensor_scalar(dst, src, mv[:, t, 0:1], rstd[:, t:t + 1],
                                                ALU.subtract, ALU.mult).then_inc(s_xn, 1)

                    def first_rest(b, t, first):
                        n = ST * b + t + 1
                        dve.wait_ge(s_part[0], n)
                        if not first or t >= 2:
                            dve.wait_ge(s_part[2], n - 2)
                        nc.vector.tensor_tensor(rest[:, t % 2], tile_at(xc, b, t), part[:, t % 2, 0],
                                                ALU.subtract).then_inc(s_rest, 1)

                    def evac(b, t):
                        b, t, n = step_of(b, t)
                        dve.wait_ge(s_turned[1], n + 2)
                        nc.vector.tensor_copy(stage_at(b, t, slice(1, 2)), psT[:, t % 2, 2:3, 0:BLK]).then_inc(s_evac[1], 1)

                    def step(b, first=False, last=False):
                        for t in range(ST):
                            ahead = not last or t + 2 < ST
                            if ahead:
                                stats(b, t + 2, first=first and t + 2 < ST)
                            if not last or t + 1 < ST:
                                norm(b, t + 1, ahead)
                            first_rest(b, t, first)
                            if not first or t >= 1:
                                evac(b, t - 1)

                    dve.wait_ge(s_id, 1)
                    stats(0, 0, first=True)
                    stats(0, 1, first=True)
                    dve.wait_ge(s_bst, 1)
                    aggregate(0)
                    norm(0, 0, True)
                    step(0, first=True)
                    with dve.Fori(1, B - 1) as b:
                        step(b)
                    step(B - 1, last=True)
                    evac(B - 1, ST - 1)

                @block.scalar
                def _(act):
                    def deviation(b, t):
                        b, t, n = step_of(b, t)
                        act.wait_ge(s_mv, n)
                        nc.scalar.activation(sdev[:, t:t + 1], mv[:, t, 1:2], ACT.Sqrt, bias=eps[:]).then_inc(s_sdev, 1)

                    def part0(b, t):
                        b, t, n = step_of(b, t)
                        act.wait_ge(s_xn, n)
                        act.wait_ge(s_turned[0], n)
                        nc.scalar.activation(part[:, t % 2, 0], tile_at(xc, b, t), ACT.Copy).then_inc(s_part[0], 1)

                    def part1(b, t):
                        act.wait_ge(s_rest, ST * b + t + 1)
                        act.wait_ge(s_turned[1], ST * b + t + 1)
                        nc.scalar.activation(part[:, t % 2, 1], rest[:, t % 2], ACT.Copy).then_inc(s_part[1], 1)

                    def evac(b, t):
                        b, t, n = step_of(b, t)
                        act.wait_ge(s_turned[0], n + 2)
                        act.wait_ge(s_turned[2], n + 2)
                        nc.scalar.activation(stage_at(b, t, slice(0, 3, 2)), psT[:, t % 2, 0:2, 0:BLK], ACT.Copy)\
                            .then_inc(s_evac[0], 1)

                    def step(b, first=False, last=False):
                        for t in range(ST):
                            if not last or t + 2 < ST:
                                deviation(b, t + 2)
                            if not last or t + 1 < ST:
                                part0(b, t + 1)
                            part1(b, t)
                            if not first or t >= 1:
                                evac(b, t - 1)

                    act.wait_ge(s_id, 1)
                    nc.scalar.activation(warm[:], eps[:], ACT.Sqrt)
                    deviation(0, 0)
                    deviation(0, 1)
                    part0(0, 0)
                    step(0, first=True)
                    with act.Fori(1, B - 1) as b:
                        step(b)
                    step(B - 1, last=True)
                    evac(B - 1, ST - 1)

                @block.tensor
                def _(pe):
                    for a in range(NPART):
                        pe.sem_inc(s_turned[a], 2)
                    for a in range(2):
                        pe.sem_inc(s_evac[a], 2)
                    pe.wait_ge(s_id, 5)
                    with pe.Fori(0, B) as b:
                        for t in range(ST):
                            for a in range(NPART):
                                pe.wait_ge(s_part[a], ST * b + t + 1)
                                pe.wait_ge(s_evac[a], ST * b + t + 1)
                                for k in range(BLK):
                                    last = nc.tensor.transpose(psT[:, t % 2, BANK[a], k], part[:, t % 2, a, k * P:(k + 1) * P],
                                                               identb[:])
                                last.then_inc(s_turned[a], 1)

        W13 = sb(whole, "W13", [P, E + 1, DC, 2, 2 * H], F16)
        W2 = sb(whole, "W2", [P, E + 1, HC, 2, D], F16)
        with ExitStack() as st:
            qs = sb(st, "qs", [P, NSLOT, G, S], BF16)
            ks = sb(st, "ks", [P, NSLOT, S], BF16)
            va = sb(st, "va", [P, NSLOT, ST, 32], F32)
            pr = sb(st, "pr", [P, 2, G, S], F32)
            ot = sb(st, "ot", [P, S], F32)
            nmax = sb(st, "nmax", [P, 2, G * ST], F32)
            nrow = sb(st, "nrow", [G * ST, 2, P], BF16)
            rec = sb(st, "rec", [P, ST, G], F32)
            wst = sb(st, "wst", [P, 2, DC * H], F32)
            w_scale = sb(st, "w_scale", [P, 1], F32)
            zrow = sb(st, "zrow", [P, ROW // 4], F32)
            ob = sb(st, "ob", [P, 2, ST, G * HD], F32)
            psS = [pb(st, f"psS{i}", [P, S], F32) for i in range(2)]
            psM = pb(st, "psM", [P, 2, 2, S], F32)
            psO = pb(st, "psO", [P, S], F32)
            psX = pb(st, "psX", [P, ST, P], F32)

            s_init = sem(st, "b_init")
            s_va = sem(st, "b_va")
            s_load = [sem(st, f"b_load{i}") for i in range(NSLOT)]
            s_row = [sem(st, f"b_row{i}") for i in range(NSLOT)]
            s_x = [sem(st, f"b_x{i}") for i in range(2)]
            s_mscore, s_nmax, s_nmaxT, s_nrow = (sem(st, f"b_{n}") for n in ("mscore", "nmax", "nmaxT", "nrow"))
            s_score, s_exp, s_pv, s_ocopy, s_oT, s_rec, s_scaled, s_out = (
                sem(st, f"b_{n}") for n in ("score", "exp", "pv", "ocopy", "oT", "rec", "scaled", "out"))
            s_w = [sem(st, f"b_w{i}") for i in range(2)]
            s_wsc, s_whi, s_wlo, s_zero, s_zd = (sem(st, f"b_{n}") for n in ("wsc", "whi", "wlo", "zero", "zd"))

            with nc.Block() as block:
                @block.sync
                def _(sp):
                    def load_unit(b, k):
                        n = k % NSLOT
                        b, k = b + k // UN, k % UN
                        for row, parts in ((0, 3), (3, 2), (5, 1)):
                            src = q_d[bass.ds(b, 1), k // 2, 0:parts, k % 2 * G * HD:(k % 2 + 1) * G * HD]
                            sp.dma_start(qs[row * HD:(row + parts) * HD, n].rearrange("r g s -> r (g s)"),
                                         src.rearrange("o a (f g) s -> (o a) f (g s)", g=G)).then_inc(s_load[n], 16)
                        src = k_d[bass.ds(b, 1), :, k * HD:(k + 1) * HD]
                        sp.dma_start(ks[0:KR, n], src.rearrange("o j f s -> (o j) f s")).then_inc(s_load[n], 16)
                        src = ctx_rows[bass.ds(b * S, S), k * HD:(k + 1) * HD]
                        sp.dma_start(va[:, n, :, 0:HD], src.rearrange("(t p) d -> p t d", p=P)).then_inc(s_load[n], 16)

                    def send_row(b, k):
                        n = k % NSLOT
                        sp.wait_ge(s_nrow, UN * b + k + 1)
                        sp.dma_start(qs[KR:KR + 1, n].rearrange("o g s -> o (g s)"), nrow[:, k % 2]).then_inc(s_row[n], 16)

                    def store(b, k):
                        kk = (k - 1) % UN
                        row0 = (b + (1 if k else 0)) * S
                        sp.wait_ge(s_out, UN * b + k + 2)
                        dst = sum_d[bass.ds(row0, S), kk * G * HD:(kk + 1) * G * HD]
                        sp.dma_start(dst.rearrange("(t p) c -> p t c", p=P), ob[:, k % 2]).then_inc(s_store[k % 2], 16)

                    def load_x(b, k, n):
                        src = x_rows[bass.ds(b * S, S), k * G * HD:(k + 1) * G * HD]
                        sp.dma_start(ob[:, n], src.rearrange("(t p) c -> p t c", p=P)).then_inc(s_x[n], 16)

                    def batch(b, last):
                        for k in range(UN):
                            n = (k + 1) % 2
                            sp.wait_ge(s_store[n], 16 * (UN // 2 * b + (k - 1) // 2 + 1) + 1)
                            load_x(b, k, n)
                            if not last or k + 1 < UN:
                                send_row(b, k + 1)
                            if not last or k + 3 < UN:
                                sp.wait_ge(s_pv, 4 * (UN * b + k) + 2)
                                load_unit(b, k + 3)
                            store(b, k)

                    for n in range(2):
                        sp.sem_inc(s_store[n], 1)
                    sp.wait_ge(s_va, 2)
                    load_unit(0, 0)
                    load_unit(0, 1)
                    load_x(0, 0, 0)
                    load_unit(0, 2)
                    sp.wait_ge(s_stored_last, STORES)
                    send_row(0, 0)
                    with sp.Fori(0, B - 1) as b:
                        batch(b, False)
                    batch(B - 1, True)
                    store(B, 0)
                    sp.wait_ge(s_store[1], 16 * (UN * B // 2) + 1)

                @block.tensor
                def _(pe):
                    def max_scores(b, k, j):
                        n, (t, g) = k % NSLOT, divmod(j, G)
                        u = UN * b + k
                        if j == 0:
                            pe.wait_ge(s_load[n], LOADS * (UN // NSLOT * b + k // NSLOT + 1))
                        if j % 2 == 0 and (k >= 1 or j >= 4):
                            pe.wait_ge(s_nmax, 8 * u + j // 2 - 1)
                        mm = nc.tensor.matmul(psM[:, j // 2 % 2, j % 2], qs[0:KR, n, g, t * P:(t + 1) * P], ks[0:KR, n],
                                              start=True, stop=True)
                        if j % 2:
                            mm.then_inc(s_mscore, 1)

                    def turn_max(b, k):
                        u = UN * b + k
                        pe.wait_ge(s_nmax, 8 * (u + 1))
                        if k >= 1:
                            pe.wait_ge(s_out, u)
                        nc.tensor.transpose(psX[0:G * ST, 0], nmax[:, k % 2], identf[:]).then_inc(s_nmaxT, 1)

                    def turn_out(b, k, row):
                        u = UN * b + k
                        pe.wait_ge(s_ocopy, u + 1)
                        if row:
                            pe.wait_ge(s_nrow, u + 2)
                        else:
                            pe.wait_ge(s_out, u + 1)
                        for t in range(ST):
                            last = nc.tensor.transpose(psX[:, t], ot[:, t * P:(t + 1) * P], identf[:])
                        last.then_inc(s_oT, 1)

                    def scores(b, k, t, g):
                        n = k % NSLOT
                        pe.wait_ge(s_exp, ST * G * (UN * b + k) + G * t + g + 1)
                        nc.tensor.matmul(psS[g % 2][:], ks[0:KR + 1, n, t * P:(t + 1) * P], qs[0:KR + 1, n, g],
                                         start=True, stop=True).then_inc(s_score, 1)

                    def values(n, t):
                        for g in range(G):
                            last = nc.tensor.matmul(psO[32 * g:32 * g + 32], va[:, n, t], pr[:, t % 2, g],
                                                    start=(t == 0), stop=(t == ST - 1))
                        last.then_inc(s_pv, 1)

                    def batch(b, last):
                        for k in range(UN):
                            n = k % NSLOT
                            pe.wait_ge(s_row[n], 16 * (UN // NSLOT * b + k // NSLOT + 1))
                            more = not last or k + 1 < UN
                            for t in range(ST):
                                scores(b, k, t, 0)
                                scores(b, k, t, 1)
                                pe.wait_ge(s_exp, ST * G * (UN * b + k) + G * t + 2)
                                if t == 0:
                                    values((k - 1) % NSLOT, ST - 1)
                                else:
                                    if t == 1:
                                        pe.wait_ge(s_ocopy, UN * b + k + 1)
                                    values(n, t - 1)
                                scores(b, k, t, 2)
                                scores(b, k, t, 3)
                                if not last or k + 2 < UN:
                                    for g in range(G):
                                        max_scores(b, k + 2, G * t + g)
                                if t == 0 and more:
                                    turn_max(b, k + 1)
                                if t == 2:
                                    turn_out(b, k, more)

                    pe.sem_inc(s_oT, 1)
                    for j in range(G * ST):
                        max_scores(0, 0, j)
                    turn_max(0, 0)
                    pe.wait_ge(s_init, 2)
                    pe.wait_ge(s_va, 2)
                    values(NSLOT - 1, 0)
                    for j in range(G * ST):
                        max_scores(0, 1, j)
                    with pe.Fori(0, B - 1) as b:
                        batch(b, False)
                    batch(B - 1, True)
                    pe.wait_ge(s_exp, ST * G * UN * B + 2)
                    values((UN - 1) % NSLOT, ST - 1)
                    turn_out(B, 0, False)

                @block.vector
                def _(dve):
                    def maximum(b, k, i):
                        u = UN * b + k
                        t, g = i // 2, i % 2 * 2
                        if i == 0 and k >= 2:
                            dve.wait_ge(s_nmaxT, u - 1)
                        dve.wait_ge(s_mscore, 8 * u + i + 1)
                        to = nmax[:, k % 2].rearrange("p (g t) -> p g t", t=ST)[:, g:g + 2, t]
                        nc.vector.tensor_reduce(to, psM[:, i % 2], AX.X, ALU.max, negate=True).then_inc(s_nmax, 1)

                    def row(b, k):
                        u = UN * b + k
                        dve.wait_ge(s_nmaxT, u + 1)
                        if k >= 2:
                            m = k - 2
                            dve.wait_ge(s_row[m % NSLOT], 16 * (UN // NSLOT * b + m // NSLOT + 1))
                        nc.vector.tensor_copy(nrow[:, k % 2], psX[0:G * ST, 0]).then_inc(s_nrow, 1)

                    def normalise(b, k):
                        u = UN * b + k
                        dve.wait_ge(s_oT, u + 2)
                        o = psX[:].rearrange("p t (g c) -> p t g c", g=G)
                        to = ob[:, k % 2].rearrange("p t (g d) -> p t g d", g=G)
                        nc.vector.reciprocal(rec[:], o[:, :, :, HD]).then_inc(s_rec, 1)
                        dve.wait_ge(s_rec, u + 1)
                        nc.vector.tensor_tensor(o[:, :, :, 0:HD], o[:, :, :, 0:HD],
                                                rec[:].unsqueeze(3).to_broadcast([P, ST, G, HD]),
                                                ALU.mult).then_inc(s_scaled, 1)
                        dve.wait_ge(s_scaled, u + 1)
                        dve.wait_ge(s_x[k % 2], 16 * (UN // 2 * b + k // 2 + 1))
                        nc.vector.tensor_tensor(to, to, o[:, :, :, 0:HD], ALU.add).then_inc(s_out, 1)

                    def batch(b, last):
                        for k in range(UN):
                            ahead = not last or k + 2 < UN
                            for i in range(8):
                                if ahead:
                                    maximum(b, k + 2, i)
                                if i == 1 and (not last or k + 1 < UN):
                                    row(b, k + 1)
                                if i == 5:
                                    normalise(b, k)

                    dve.sem_inc(s_out, 1)
                    nc.vector.memset(va[:], 0.0).then_inc(s_va, 1)
                    dve.wait_ge(s_va, 1)
                    nc.vector.memset(va[:, :, :, HD:HD + 1], 1.0).then_inc(s_va, 1)
                    for i in range(8):
                        maximum(0, 0, i)
                    row(0, 0)
                    for i in range(8):
                        maximum(0, 1, i)
                    with dve.Fori(0, B - 1) as b:
                        batch(b, False)
                    batch(B - 1, True)
                    normalise(B, 0)

                @block.scalar
                def _(act):
                    def exps(b, k, t, g):
                        u = UN * b + k
                        act.wait_ge(s_score, ST * G * u + G * t + g + 1)
                        if g == 0:
                            act.wait_ge(s_pv, ST * u + t + 1)
                        nc.scalar.activation(pr[:, t % 2, g], psS[g % 2][:], ACT.Exp, scale=SCALE).then_inc(s_exp, 1)

                    def copy_out(b, k):
                        u = UN * b + k
                        act.wait_ge(s_pv, ST * u + 2)
                        act.wait_ge(s_oT, u + 1)
                        nc.scalar.activation(ot[:], psO[:], ACT.Copy).then_inc(s_ocopy, 1)

                    def batch(b):
                        for k in range(UN):
                            for t in range(ST):
                                for g in range(G):
                                    exps(b, k, t, g)
                                if t == 0:
                                    copy_out(b, k)

                    nc.scalar.activation(rec[:], identf[:, 0:ST * G].rearrange("p (t g) -> p t g", g=G), ACT.Exp).then_inc(s_exp, 2)
                    with act.Fori(0, B) as b:
                        batch(b)
                    copy_out(B, 0)

                @block.gpsimd
                def _(pool):
                    nc.gpsimd.memset(ks[KR:KR + 1], 1.0).then_inc(s_init, 1)
                    pool.wait_ge(s_init, 1)
                    nc.gpsimd.memset(pr[:], 1.0).then_inc(s_init, 1)
                    pool.wait_ge(s_init, 2)
                    nc.gpsimd.memset(zrow[:], 0.0).then_inc(s_zero, 1)
                    nc.gpsimd.memset(wst[:], 0.0).then_inc(s_zero, 1)
                    nc.gpsimd.memset(w_scale[:], W_SCALE).then_inc(s_zero, 1)
                    pool.wait_ge(s_zero, 3)

                    def split(i, src, hi, lo):
                        c = w_scale[0:src.shape[0]]
                        if len(src.shape) == 3:
                            c = c.unsqueeze(2)
                        c = c.to_broadcast(list(src.shape))
                        nc.gpsimd.tensor_tensor(hi, src, c, ALU.mult).then_inc(s_whi, 1)
                        nc.gpsimd.tensor_tensor(src, src, c, ALU.mult).then_inc(s_wsc, 1)
                        pool.wait_ge(s_whi, i + 1)
                        pool.wait_ge(s_wsc, i + 1)
                        nc.gpsimd.tensor_tensor(lo, src, hi, ALU.subtract).then_inc(s_wlo, 1)

                    def expert(e, w1e, w3e, w2e, slot):
                        full = (HC - 1) * P
                        for half, w in enumerate((w1e, w3e)):
                            pool.wait_ge(s_zero, 3)
                            pool.wait_ge(s_wlo, 4 * e)
                            src = wst[:, half].rearrange("p (c h) -> p c h", h=H)
                            pool.dma_start(src, w.rearrange("(c p) h -> p c h", p=P)).then_inc(s_w[half], 16)
                        for half in range(2):
                            pool.wait_ge(s_w[half], 32 * e + 16)
                            dst = W13[:, slot, :, :, half * H:(half + 1) * H]
                            split(4 * e + half, wst[:, half].rearrange("p (c h) -> p c h", h=H),
                                  fold(dst[..., 0, :]), fold(dst[..., 1, :]))
                        pool.wait_ge(s_zero, 3)
                        pool.wait_ge(s_wlo, 4 * e + 2)
                        pool.dma_start(wst[:, 0, 0:(HC - 1) * D].rearrange("p (c d) -> p c d", d=D),
                                       w2e[0:full].rearrange("(c p) d -> p c d", p=P)).then_inc(s_w[0], 16)
                        pool.dma_start(wst[0:HL, 1, 0:D], w2e[full:H]).then_inc(s_w[1], 16)
                        pool.wait_ge(s_w[0], 32 * e + 32)
                        split(4 * e + 2, wst[:, 0, 0:(HC - 1) * D].rearrange("p (c d) -> p c d", d=D),
                              fold(W2[:, slot, 0:HC - 1, 0]), fold(W2[:, slot, 0:HC - 1, 1]))
                        pool.wait_ge(s_w[1], 32 * e + 32)
                        split(4 * e + 3, wst[0:HL, 1:2, 0:D], fold(W2[0:HL, slot, HC - 1:HC, 0]),
                              fold(W2[0:HL, slot, HC - 1:HC, 1]))

                    def fold(ap):
                        return ap.squeeze(1) if len(ap.shape) == 4 else ap

                    pool.wait_ge(s_row[0], 16)
                    pool.wait_ge(s_stored_last, STORES)
                    expert(0, sw1, sw3, sw2, E)
                    for c in range(4):
                        pool.dma_start(sum_d[S + N:, c * P:(c + 1) * P], zrow[:, 0:P]).then_inc(s_zd, 16)
                    cq = ROW // 4

                    def fill(e, c):
                        share = SHARE * P
                        pool.dma_start(xs_d[bass.ds(N + e * share, share), c * cq:(c + 1) * cq].rearrange("(t p) c -> p t c", p=P),
                                       zrow[:].unsqueeze(1).to_broadcast([P, SHARE, cq])).then_inc(s_zd, 16)

                    with pool.Fori(0, E) as e:
                        one = bass.ds(e, 1)
                        expert(e + 1, w1[one].squeeze(0), w3[one].squeeze(0), w2[one].squeeze(0), one)
                        for c in range(3):
                            fill(e, c)
                    pool.wait_ge(s_zd, 16 * (4 + 3 * E))
                    nc.gpsimd.iota(zrow[:, D + 1 - 3 * cq:D + 2 - 3 * cq], [[0, 1]], base=S + N, channel_multiplier=1,
                                   allow_small_or_imprecise_dtypes=True).then_inc(s_zero, 1)
                    pool.wait_ge(s_zero, 4)
                    with pool.Fori(0, E) as e:
                        fill(e, 3)
                    pool.wait_ge(s_wlo, 4 * (E + 1))
                    pool.wait_ge(s_zd, 16 * (4 + 4 * E))

        with ExitStack() as st_cd:
            slot_i = sb(st_cd, "slot_i", [P, TOP_K, NT], I32)
            tile_w = sb(st_cd, "tile_w", [P, WORDS], I32)
            wts = sb(st_cd, "wts", [P, TOP_K, NT], F32)
            iota_t = sb(st_cd, "iota_t", [P, RT], F32)
            KEPT = 3
            xr = sb(st_cd, "xr", [P, NT, ROW], F32)
            kept = xr[:, NT - KEPT:NT].rearrange("p t c -> p (t c)")
            taken = [0]

            def work(*shape):
                n = 1
                for size in shape:
                    n *= size
                a = kept[:, taken[0]:taken[0] + n]
                taken[0] += n
                assert taken[0] <= KEPT * ROW
                if len(shape) == 2:
                    return a.rearrange("p (a b) -> p a b", a=shape[0])
                if len(shape) == 3:
                    return a.rearrange("p (a b c) -> p a b c", a=shape[0], b=shape[1])
                return a

            pick = work(TOP_K, NT * E).rearrange("p k (t e) -> p k t e", e=E)
            cum = work(2, NT + 1, E)
            cnt_i = work(2, E).bitcast(I32)
            padf = work(E)
            base = work(2, E + 1)
            slots = work(NT, E)
            hit = work(NT, E)
            slotf = work(TOP_K, NT)
            past = work(RT, E)
            tef = work(TILES + 8)
            words = work(WORDS)
            psC = [pb(st_cd, f"psC{i}", [P, NT, E], F32) for i in range(2)]
            with ExitStack() as st:
                xn = sb(st, "xn", [P, ST, ROW], F32)
                bst = sb(st, "bst2", [P, ST, 6], F32)
                mv = sb(st, "mv2", [P, ST, 2], F32)
                eps = sb(st, "eps2", [P, 1], F32)
                warm = sb(st, "warm2", [P, 1], F32)
                sdev = sb(st, "sdev2", [P, ST], F32)
                rstd = sb(st, "rstd2", [P, ST], F32)
                xT = sb(st, "xT", [P, 2, DC, P], F32)
                gw = xr[0:E, NT - 1, 0:D]
                gwT = sb(st, "gwT", [P, DC, E], F32)
                lgT = xr[0:E, :, 0:D]
                sc = sb(st, "sc", [P, NT, E], F32)
                mx = sb(st, "mx", [P, NT, 8], F32)
                ix = sb(st, "ix", [P, NT, 8], U32)
                ixf = sb(st, "ixf", [P, NT, TOP_K], F32)
                iota_e = sb(st, "iota_e", [P, NT, E], F32)
                before = sb(st, "before", [P, P], F32)
                ones = sb(st, "ones", [P, P], F32)
                both = sb(st, "both", [P, NT, E], F32)
                den = sb(st, "den", [P, 2, NT], F32)
                psT = [pb(st, f"psT2{i}", [P, DC, P], F32) for i in range(2)]
                psL = [pb(st, f"psL{i}", [E, P], F32) for i in range(2)]
                psR = pb(st, "psR", [P, NT, E], F32)
                psG = pb(st, "psG", [P, DC, E], F32)

                s_x = [sem(st, f"c_in{i}") for i in range(ST)]
                s_row = [sem(st, f"c_row{i}") for i in range(ST)]
                s_gw = sem(st, "c_gw")
                s_cst, s_gT, s_gwT, s_bst, s_mv, s_sdev, s_rstd, s_xn = (
                    sem(st, f"c_{n}") for n in ("cst", "gT", "gwT", "bst", "mv", "sdev", "rstd", "xn"))
                s_xTp, s_xT, s_log, s_lg, s_back, s_sc, s_both, s_count, s_v = (
                    sem(st, f"c_{n}") for n in ("xTp", "xT", "log", "lg", "back", "sc", "both", "count", "v"))

                with nc.Block() as block:
                    @block.sync
                    def _(sp):
                        def load(b, t):
                            sp.dma_start(xr[:, bass.ds(ST * b + t, 1), 0:D].rearrange("p o d -> p (o d)"),
                                         sum_d[bass.ds(b * S + t * P + S, P), :]).then_inc(s_x[t], 16)

                        def store(b, t):
                            b, t = b + t // ST, t % ST
                            sp.wait_ge(s_xn, ST * b + t + 1)
                            sp.dma_start(xs_d[bass.ds(b * S + t * P, P), :], xn[:, t]).then_inc(s_row[t], 16)

                        def step(b, first=False, last=False):
                            for t in range(ST):
                                if not last:
                                    sp.wait_ge(s_bst, ST * b + t + 1)
                                    load(b + 1, t)
                                if not first or t >= 2:
                                    store(b, t - 2)

                        for t in range(ST):
                            sp.sem_inc(s_row[t], 1)
                            load(0, t)
                        sp.dma_start(gw, gate_w).then_inc(s_gw, 16)
                        sp.wait_ge(s_store[0], 16 * (UN * B // 2 + 1) + 1)
                        step(0, first=True)
                        with sp.Fori(1, B - 1) as b:
                            step(b)
                        step(B - 1, last=True)
                        store(B - 1, ST - 2)
                        store(B - 1, ST - 1)
                        for t in range(ST):
                            sp.wait_ge(s_row[t], 16 * B + 1)

                    @block.gpsimd
                    def _(pool):
                        nc.gpsimd.memset(eps[:], LN_EPS).then_inc(s_cst, 1)
                        pool.wait_ge(s_cst, 1)
                        nc.gpsimd.iota(iota_e[:], [[0, NT], [1, E]], base=0, channel_multiplier=0,
                                       allow_small_or_imprecise_dtypes=True).then_inc(s_cst, 1)
                        nc.gpsimd.iota(iota_t[:], [[P, RT]], base=0, channel_multiplier=0,
                                       allow_small_or_imprecise_dtypes=True).then_inc(s_cst, 1)
                        nc.gpsimd.memset(ones[:], 1.0).then_inc(s_cst, 1)
                        pool.wait_ge(s_cst, 4)
                        nc.gpsimd.affine_select(out=before[:], in_=ones[:], compare_op=ALU.is_gt, fill=0.0, base=0,
                                                pattern=[[1, P]], channel_multiplier=-1).then_inc(s_cst, 1)
                        nc.gpsimd.memset(xn[:, :, D:ROW], 1.0 / (W_SCALE * G_SCALE)).then_inc(s_cst, 1)
                        pool.wait_ge(s_cst, 6)
                        nc.gpsimd.iota(xn[:, :, D + 1:D + 2], [[P, ST], [0, 1]], base=0, channel_multiplier=1,
                                       allow_small_or_imprecise_dtypes=True).then_inc(s_cst, 1)

                    @block.scalar
                    def _(act):
                        act.sem_inc(s_xT, 2)
                        act.sem_inc(s_lg, 2)
                        act.wait_ge(s_cst, 1)
                        nc.scalar.activation(warm[:], eps[:], ACT.Sqrt)

                        def deviation(b, t):
                            act.wait_ge(s_mv, ST * b + t + 1)
                            nc.scalar.activation(sdev[:, t:t + 1], mv[:, t, 1:2], ACT.Sqrt, bias=eps[:]).then_inc(s_sdev, 1)

                        def take_logits(b, t):
                            act.wait_ge(s_log, ST * b + t + 3)
                            nc.scalar.activation(lgT[:, bass.ds(b, 1), t * P:(t + 1) * P].rearrange("p o d -> p (o d)"),
                                                 psL[t % 2][:], ACT.Copy).then_inc(s_lg, 1)

                        def step(b, first=False, last=False):
                            for t in range(ST):
                                if not last or t + 2 < ST:
                                    deviation(b + (t + 2) // ST, (t + 2) % ST)
                                if t > 1 or not first:
                                    take_logits(b + (t - 2) // ST, (t - 2) % ST)
                                act.wait_ge(s_xTp, ST * b + t + 1)
                                act.wait_ge(s_log, ST * b + t + 1)
                                nc.scalar.activation(xT[:, t % 2], psT[t % 2][:], ACT.Copy).then_inc(s_xT, 1)

                        deviation(0, 0)
                        deviation(0, 1)
                        step(0, first=True)
                        with act.Fori(1, B - 1) as b:
                            step(b)
                        step(B - 1, last=True)
                        nc.scalar.activation(warm[:], eps[:], ACT.Sigmoid)
                        take_logits(B - 1, ST - 2)
                        take_logits(B - 1, ST - 1)
                        act.wait_ge(s_back, 1)
                        nc.scalar.activation(sc[:], psR[:], ACT.Sigmoid).then_inc(s_sc, 1)

                    @block.tensor
                    def _(pe):
                        pe.wait_ge(s_gw, 16)
                        for c in range(DC):
                            last = nc.tensor.transpose(psG[:, c], gw[:, c * P:(c + 1) * P], identf[0:E, 0:E])
                        last.then_inc(s_gT, 1)
                        pe.wait_ge(s_gwT, 1)

                        pe.sem_inc(s_log, 2)

                        def turn(b, t):
                            pe.wait_ge(s_xn, ST * b + t + 1)
                            pe.wait_ge(s_xT, ST * b + t + 1)
                            for c in range(DC):
                                last = nc.tensor.transpose(psT[t % 2][:, c], xn[:, t, c * P:(c + 1) * P], identf[:])
                            last.then_inc(s_xTp, 1)

                        def logits(b, t):
                            pe.wait_ge(s_xT, ST * b + t + 3)
                            pe.wait_ge(s_lg, ST * b + t + 1)
                            for c in range(DC):
                                last = nc.tensor.matmul(psL[t % 2][:], gwT[:, c], xT[:, t % 2, c], start=(c == 0),
                                                        stop=(c == DC - 1))
                            last.then_inc(s_log, 1)

                        with pe.Fori(0, B) as b:
                            for t in range(ST):
                                turn(b, t)
                                if t:
                                    logits(b, t - 1)
                            logits(b, ST - 1)
                        pe.wait_ge(s_lg, NT + 2)
                        for i in range(NT):
                            last = nc.tensor.transpose(psR[:, i], lgT[:, i // ST, i % ST * P:(i % ST + 1) * P], identf[0:E, 0:E])
                        last.then_inc(s_back, 1)
                        pe.wait_ge(s_cst, 5)
                        pe.wait_ge(s_both, 1)
                        nc.tensor.matmul(psC[0][:].rearrange("p t e -> p (t e)"), before[:],
                                         both[:].rearrange("p t e -> p (t e)"), start=True, stop=True)
                        nc.tensor.matmul(psC[1][:].rearrange("p t e -> p (t e)"), ones[:],
                                         both[:].rearrange("p t e -> p (t e)"), start=True, stop=True).then_inc(s_count, 1)

                    @block.vector
                    def _(dve):
                        steps = [0]

                        def then(ins):
                            steps[0] += 1
                            ins.then_inc(s_v, 1)
                            dve.wait_ge(s_v, steps[0])

                        dve.wait_ge(s_cst, 7)

                        def stats(b, t):
                            b, t = b + t // ST, t % ST
                            dve.wait_ge(s_x[t], 16 * b + 16)
                            nc.vector.bn_stats(bst[:, t], xr[:, bass.ds(ST * b + t, 1), 0:D].rearrange("p o d -> p (o d)"))\
                                .then_inc(s_bst, 1)

                        def aggregate(t):
                            nc.vector.bn_aggr(mv[:, t % ST], bst[:, t % ST]).then_inc(s_mv, 1)

                        def norm(b, t):
                            dve.wait_ge(s_rstd, ST * b + t + 1)
                            dve.wait_ge(s_row[t], 16 * b + 1)
                            nc.vector.tensor_scalar(xn[:, t, 0:D], xr[:, bass.ds(ST * b + t, 1), 0:D].rearrange("p o d -> p (o d)"),
                                                    mv[:, t, 0:1], rstd[:, t:t + 1], ALU.subtract, ALU.mult)
                            nc.vector.tensor_scalar_add(xn[:, t, D + 1:D + 2], xn[:, t, D + 1:D + 2], float(S)).then_inc(s_xn, 1)

                        def step(b, last=False):
                            for t in range(ST):
                                ahead = not last or t + 2 < ST
                                if ahead:
                                    stats(b, t + 2)
                                dve.wait_ge(s_sdev, ST * b + t + 1)
                                if ahead:
                                    dve.wait_ge(s_bst, ST * b + t + 3)
                                nc.vector.reciprocal(rstd[:, t:t + 1], sdev[:, t:t + 1]).then_inc(s_rstd, 1)
                                if ahead:
                                    aggregate(t + 2)
                                norm(b, t)

                        stats(0, 0)
                        stats(0, 1)
                        dve.wait_ge(s_bst, 2)
                        aggregate(0)
                        aggregate(1)
                        dve.wait_ge(s_gT, 1)
                        nc.vector.tensor_copy(gwT[:], psG[:]).then_inc(s_gwT, 1)
                        with dve.Fori(0, B - 1) as b:
                            step(b)
                        step(B - 1, last=True)
                        dve.wait_ge(s_sc, 1)
                        for t in range(NT):
                            last = nc.vector.max(mx[:, t], sc[:, t])
                        then(last)
                        for t in range(NT):
                            last = nc.vector.max_index(ix[:, t], mx[:, t], sc[:, t])
                        then(last)
                        then(nc.vector.tensor_copy(ixf[:], ix[:, :, 0:TOP_K]))
                        dve.wait_ge(s_cst, 5)
                        for k in range(TOP_K):
                            then(nc.vector.tensor_tensor(pick[:, k], iota_e[:], ixf[:, :, k:k + 1].to_broadcast([P, NT, E]),
                                                         ALU.is_equal))
                        nc.vector.tensor_tensor(both[:], pick[:, 0], pick[:, 1], ALU.add).then_inc(s_both, 1)
                        then(nc.vector.tensor_tensor(den[:, 0], mx[:, :, 0], mx[:, :, 1], ALU.add))
                        then(nc.vector.tensor_scalar_add(den[:, 0], den[:, 0], 1e-20))
                        then(nc.vector.reciprocal(den[:, 1], den[:, 0]))
                        for k in range(TOP_K):
                            then(nc.vector.tensor_tensor(wts[:, k], mx[:, :, k], den[:, 1], ALU.mult))
                        then(nc.vector.tensor_scalar_mul(wts[:], wts[:], ROUTED_SCALE / (W_SCALE * G_SCALE)))

            with ExitStack() as st:
                xt = sb(st, "xt", [P, 2, ROW], F32)
                xh = sb(st, "xh", [P, 2, DC, P], F16)
                xl = sb(st, "xl", [P, 2, DC, P], F16)
                sg = sb(st, "sg", [P, 2, H], F32)
                gg = sb(st, "gg", [P, 2, HC * P], F32)
                gh = sb(st, "gh", [P, 2, HC, P], F16)
                gl = sb(st, "gl", [P, 2, HC, P], F16)
                yo = sb(st, "yo", [P, 2, D], F32)
                wtc = sb(st, "wtc", [P, 2, 1], F32)
                warm = sb(st, "warm3", [P, 1], F32)
                num = sb(st, "num", [P, 2, 1], I32)
                psXT = pb(st, "psXT", [P, DC, P], F32)
                psH = pb(st, "psH", [P, 512], F32)
                psU = pb(st, "psU", [P, 512], F32)
                psGT = pb(st, "psGT", [P, HC, P], F32)
                psY = [pb(st, f"psY{i}", [P, D], F32) for i in range(2)]
                s_init = sem(st, "d_init")
                s_step, s_slots, s_words = (sem(st, f"d_{n}") for n in ("step", "slots", "words"))
                s_xr, s_xrn, s_xrw, s_sent, s_added, s_num, s_done = (
                    sem(st, f"d_{n}") for n in ("xr", "xrn", "xrw", "sent", "added", "num", "done"))
                s_xt = [sem(st, f"d_xt{i}") for i in range(2)]
                s_xT, s_xh, s_xl, s_hu, s_sg, s_g, s_gT, s_gh, s_gl, s_y, s_yo, s_wt = (
                    sem(st, f"d_{n}") for n in ("xT", "xh", "xl", "hu", "sg", "g", "gT", "gh", "gl", "y", "yo", "wt"))

                with nc.Block() as block:
                    @block.sync
                    def _(sp):
                        def load(i, j, shift=0):
                            sp.dma_start(xt[:, j], xs_d[bass.ds((i + shift) * P, P), :]).then_inc(s_xt[j], 16)

                        def next_load(i, j, shift):
                            sp.wait_ge(s_xT, i + 1)
                            sp.wait_ge(s_wt, i + 1)
                            sp.wait_ge(s_num, i + 1)
                            load(i + 2, j, shift)

                        def next_loads(lo, hi, shift):
                            i = lo - 2
                            if i % 2:
                                next_load(i, 1, shift)
                                i += 1
                            with sp.Fori(i // 2, (hi - 2) // 2) as m:
                                for j in range(2):
                                    next_load(2 * m + j, j, shift)
                            if hi % 2:
                                next_load(hi - 3, 0, shift)

                        def copy_out(lo, hi, after):
                            sp.wait_ge(s_added, 16 * (after + 1))
                            sp.dma_start(out_rows[lo * P:hi * P], sum_d[S + lo * P:S + hi * P]).then_inc(s_done, 16)

                        load(0, 0)
                        load(1, 1)
                        rows = xs_d[0:N].rearrange("(t p) c -> p t c", p=P)
                        sp.dma_start(xr[:, 0:NT - KEPT], rows[:, 0:NT - KEPT]).then_inc(s_xr, 16)
                        sp.wait_ge(s_slots, 1)
                        sp.wait_ge(s_words, 1)
                        sp.dma_start(xr[:, NT - KEPT:NT], rows[:, NT - KEPT:NT]).then_inc(s_xr, 16)
                        next_loads(2, FIRST, 0)
                        sp.wait_ge(s_sent, 16 * NT * TOP_K)
                        next_loads(FIRST, FIRST + RT, NT - FIRST)
                        for i in range(FIRST + RT - 2, TILES - 2):
                            next_load(i, i % 2, -RT)
                        for n in range(LAST):
                            copy_out(n * FIRST // LAST, (n + 1) * FIRST // LAST, FIRST + RT - 1 + n)
                            if n:
                                copy_out(FIRST + n - 1, FIRST + n, FIRST + RT - 1 + n)
                        copy_out(NT - 1, NT, TILES - 1)
                        sp.wait_ge(s_done, 16 * 2 * LAST)

                    @block.gpsimd
                    def _(pool):
                        def add(i):
                            pool.wait_ge(s_yo, i + 1)
                            pool.wait_ge(s_num, i + 1)
                            if i:
                                pool.wait_ge(s_added, 16 * i)
                            nc.gpsimd.indirect_dma_start(
                                out=sum_d, out_offset=bass.IndirectOffsetOnAxis(ap=num[:, i % 2].bitcast(U32), axis=0),
                                in_=yo[:, i % 2], in_offset=None, compute_op=ALU.add).then_inc(s_added, 16)

                        pool.wait_ge(s_xr, 32)
                        pool.wait_ge(s_slots, 1)
                        added = 0
                        for k in range(TOP_K):
                            if k:
                                pool.wait_ge(s_sent, 16 * NT * k)
                            nc.gpsimd.tensor_copy(xr[:, :, D:D + 1], wts[:, k].unsqueeze(2)).then_inc(s_xrw, 1)
                            if not k:
                                nc.gpsimd.iota(xr[:, :, D + 1:D + 2], [[P, NT], [0, 1]], base=S, channel_multiplier=1,
                                               allow_small_or_imprecise_dtypes=True).then_inc(s_xrn, 1)
                                pool.wait_ge(s_xrn, 1)
                            pool.wait_ge(s_xrw, k + 1)
                            for t in range(NT):
                                nc.gpsimd.indirect_dma_start(
                                    out=xs_d, out_offset=bass.IndirectOffsetOnAxis(ap=slot_i[:, k, t:t + 1].bitcast(U32), axis=0),
                                    in_=xr[:, t], in_offset=None).then_inc(s_sent, 16)
                                if t % 4 == 3:
                                    add(added)
                                    added += 1
                        for i in range(added, TILES):
                            add(i)
                        pool.wait_ge(s_added, 16 * TILES)

                    @block.tensor
                    def _(pe):
                        def experts_of(m, count):
                            word = pe.value_load(tile_w[0:1, bass.ds(m, 1)], min_val=0, max_val=16 ** AHEAD - 1)
                            return [pe.snap(((word >> (4 * n)) & 15).with_bounds(min_val=0, max_val=E)) for n in range(count)]

                        def turn_x(i, j, half):
                            pe.wait_ge(s_xt[j], 16 * half + 16)
                            pe.wait_ge(s_xh, i)
                            pe.wait_ge(s_xl, i)
                            for c in range(DC):
                                last = nc.tensor.transpose(psXT[:, c], xt[:, j, c * P:(c + 1) * P], identf[:])
                            last.then_inc(s_xT, 1)

                        def up(i, j, e):
                            pe.wait_ge(s_xh, i + 1)
                            pe.wait_ge(s_xl, i + 1)
                            pe.wait_ge(s_g, i)
                            n = 0
                            for c in range(DC):
                                for xp, wp in ((xh, 0), (xh, 1), (xl, 0)):
                                    for ps, at in ((psH, 0), (psU, H)):
                                        last = nc.tensor.matmul(
                                            ps[:, 0:H], xp[:, j, c],
                                            W13[:, bass.ds(e, 1), c, wp, at:at + H].rearrange("p o h -> p (o h)"),
                                            start=(n == 0), stop=(n == 3 * DC - 1))
                                    n += 1
                            last.then_inc(s_hu, 1)

                        def turn_g(i, j):
                            pe.wait_ge(s_g, i + 1)
                            pe.wait_ge(s_gh, i)
                            pe.wait_ge(s_gl, i)
                            for c in range(HC):
                                last = nc.tensor.transpose(psGT[:, c], gg[:, j, c * P:(c + 1) * P], identf[:])
                            last.then_inc(s_gT, 1)

                        def down(i, j, e):
                            pe.wait_ge(s_gh, i + 1)
                            pe.wait_ge(s_gl, i + 1)
                            if not isinstance(i, int) or i >= 2:
                                pe.wait_ge(s_yo, i - 1)
                            n = 0
                            for c in range(HC):
                                rows = P if c < HC - 1 else HL
                                for gp, wp in ((gh, 0), (gh, 1), (gl, 0)):
                                    last = nc.tensor.matmul(
                                        psY[j][:], gp[0:rows, j, c],
                                        W2[0:rows, bass.ds(e, 1), c, wp, :].rearrange("p o d -> p (o d)"),
                                        start=(n == 0), stop=(n == 3 * HC - 1))
                                    n += 1
                            last.then_inc(s_y, 1)

                        turn_x(0, 0, 0)
                        up(0, 0, E)
                        turn_x(1, 1, 0)
                        turn_g(0, 0)
                        up(1, 1, E)
                        turn_x(2, 0, 1)
                        down(0, 0, E)
                        turn_g(1, 1)
                        up(2, 0, E)
                        turn_x(3, 1, 1)
                        down(1, 1, E)
                        turn_g(2, 0)
                        def four(m, last=False):
                            e = experts_of(m, AHEAD)
                            for n in range(2, AHEAD + 1):
                                i = 4 * m + n
                                up(i + 1, (n + 1) % 2, e[n - 1])
                                if not last or i + 2 < TILES:
                                    turn_x(i + 2, n % 2, 2 * m + (n + 2) // 2)
                                down(i, n % 2, e[n - 2])
                                turn_g(i + 1, (n + 1) % 2)
                            if last:
                                down(TILES - 1, 0, e[AHEAD - 1])

                        pe.wait_ge(s_words, 1)
                        with pe.Fori(0, TILES // 4 - 1) as m:
                            four(m)
                        four(TILES // 4 - 1, last=True)

                    @block.scalar
                    def _(act):
                        def split_x(i, j):
                            act.wait_ge(s_xT, i + 1)
                            if not isinstance(i, int) or i >= 2:
                                act.wait_ge(s_hu, i - 1)
                            nc.scalar.activation(xh[:, j], psXT[:], ACT.Copy).then_inc(s_xh, 1)

                        def silu(i, j):
                            act.wait_ge(s_hu, i + 1)
                            nc.scalar.activation(sg[:, j], psH[:, 0:H], ACT.Silu, scale=1.0 / W_SCALE).then_inc(s_sg, 1)

                        def split_g(i, j):
                            act.wait_ge(s_gT, i + 1)
                            if not isinstance(i, int) or i >= 2:
                                act.wait_ge(s_y, i - 1)
                            nc.scalar.activation(gh[:, j], psGT[:], ACT.Copy).then_inc(s_gh, 1)

                        def result(i, j):
                            act.wait_ge(s_y, i + 1)
                            act.wait_ge(s_wt, i + 1)
                            if not isinstance(i, int) or i >= 2:
                                act.wait_ge(s_added, 16 * (i - 1))
                            nc.scalar.activation(yo[:, j], psY[j][:], ACT.Copy, scale=wtc[:, j]).then_inc(s_yo, 1)

                        def tile(i, j, first=False, last=False):
                            silu(i, j)
                            if not last:
                                split_x(i + 1, 1 - j)
                            if not first:
                                result(i - 1, 1 - j)
                            split_g(i, j)

                        nc.scalar.activation(warm[:], identf[:, 0:1], ACT.Silu)
                        split_x(0, 0)
                        tile(0, 0, first=True)
                        tile(1, 1)
                        tile(2, 0)
                        tile(3, 1)
                        with act.Fori(2, TILES // 2) as m:
                            tile(2 * m, 0)
                            tile(2 * m + 1, 1)
                        tile(TILES - 1, 0, last=True)
                        result(TILES - 1, 0)

                    @block.vector
                    def _(dve):
                        steps = [0]

                        def then(ins):
                            steps[0] += 1
                            ins.then_inc(s_step, 1)
                            dve.wait_ge(s_step, steps[0])

                        def running_sum(two, count):
                            at, by = 0, 1
                            while by < count:
                                nc.vector.tensor_copy(two[:, 1 - at, 1:by + 1], two[:, at, 1:by + 1])
                                then(nc.vector.tensor_tensor(two[:, 1 - at, by + 1:], two[:, at, by + 1:],
                                                             two[:, at, 1:count + 1 - by], ALU.add))
                                at, by = 1 - at, 2 * by
                            return at

                        def find_first_slots():
                            then(nc.vector.memset(cum[:, :, 0], 0.0))
                            then(nc.vector.tensor_copy(cum[:, 0, 1:], psC[1][:]))
                            at = running_sum(cum, NT)
                            then(nc.vector.tensor_scalar_add(padf[:], cum[:, at, NT], float(P - 1)))
                            then(nc.vector.tensor_copy(cnt_i[:, 0], padf[:]))
                            then(nc.vector.tensor_single_scalar(cnt_i[:, 1], cnt_i[:, 0], P.bit_length() - 1, ALU.arith_shift_right))
                            then(nc.vector.tensor_copy(padf[:], cnt_i[:, 1]))
                            then(nc.vector.memset(base[:, :, 0:1], 0.0))
                            then(nc.vector.tensor_scalar_mul(base[:, 0, 1:], padf[:], float(P)))
                            return at, base[:, running_sum(base, E)]

                        def find_slots(at, first):
                            then(nc.vector.tensor_tensor(slots[:], cum[:, at, 0:NT], psC[0][:], ALU.add))
                            then(nc.vector.tensor_tensor(slots[:], slots[:], first[:, 0:E].unsqueeze(1).to_broadcast([P, NT, E]), ALU.add))
                            for k in range(TOP_K):
                                then(nc.vector.tensor_tensor(hit[:], slots[:], pick[:, k], ALU.mult))
                                then(nc.vector.tensor_reduce(slotf[:, k], hit[:], AX.X, ALU.add))
                            then(nc.vector.tensor_scalar_add(slotf[:], slotf[:], float(N)))
                            nc.vector.tensor_copy(slot_i[:], slotf[:]).then_inc(s_slots, 1)

                        def find_tile_experts(first):
                            then(nc.vector.tensor_tensor(past[:], iota_t[:].unsqueeze(2).to_broadcast([P, RT, E]),
                                                         first[:, 1:E + 1].unsqueeze(1).to_broadcast([P, RT, E]), ALU.is_ge))
                            then(nc.vector.memset(tef[:], float(E)))
                            routed = tef[:, FIRST:FIRST + RT]
                            then(nc.vector.tensor_reduce(routed, past[:], AX.X, ALU.add))
                            then(nc.vector.tensor_scalar_min(routed, routed, float(E - 1)))
                            then(nc.vector.tensor_copy(words[:], tef[:, 2:TILES + 2:4]))
                            for n in range(1, AHEAD):
                                then(nc.vector.scalar_tensor_tensor(words[:], tef[:, 2 + n:TILES + 2 + n:4], 16.0 ** n, words[:],
                                                                    ALU.mult, ALU.add))
                            nc.vector.tensor_copy(tile_w[:], words[:]).then_inc(s_words, 1)

                        def split_x(i, j):
                            dve.wait_ge(s_xh, i + 1)
                            nc.vector.tensor_tensor(xl[:, j], psXT[:], xh[:, j], ALU.subtract).then_inc(s_xl, 1)

                        def gate(i, j):
                            dve.wait_ge(s_sg, i + 1)
                            if not isinstance(i, int) or i >= 2:
                                dve.wait_ge(s_gT, i - 1)
                            nc.vector.scalar_tensor_tensor(gg[:, j, 0:H], psU[:, 0:H], G_SCALE / W_SCALE, sg[:, j],
                                                           ALU.mult, ALU.mult).then_inc(s_g, 1)

                        def split_g(i, j):
                            dve.wait_ge(s_gh, i + 1)
                            nc.vector.tensor_tensor(gl[:, j], psGT[:], gh[:, j], ALU.subtract).then_inc(s_gl, 1)

                        def take_row_end(i, j, half):
                            dve.wait_ge(s_xt[j], 16 * half + 16)
                            if not isinstance(i, int) or i >= 2:
                                dve.wait_ge(s_yo, i - 1)
                            nc.vector.tensor_copy(wtc[:, j], xt[:, j, D:D + 1]).then_inc(s_wt, 1)
                            if not isinstance(i, int) or i >= 2:
                                dve.wait_ge(s_added, 16 * (i - 1))
                            nc.vector.tensor_copy(num[:, j], xt[:, j, D + 1:D + 2]).then_inc(s_num, 1)

                        def tile(i, j, half, last=False):
                            gate(i, j)
                            if not last:
                                split_x(i + 1, 1 - j)
                            split_g(i, j)
                            if not last:
                                take_row_end(i + 1, 1 - j, half + 1 if j else half)

                        at, first = find_first_slots()
                        split_x(0, 0)
                        take_row_end(0, 0, 0)
                        nc.vector.memset(gg[:], 0.0).then_inc(s_init, 1)
                        find_slots(at, first)
                        dve.wait_ge(s_init, 1)
                        find_tile_experts(first)
                        tile(0, 0, 0)
                        tile(1, 1, 0)
                        with dve.Fori(1, TILES // 2) as m:
                            tile(2 * m, 0, m)
                            tile(2 * m + 1, 1, m)
                        tile(TILES - 1, 0, TILES // 2, last=True)


_INS = ["x", "ctx_512", "L0_ffn_gate_w", "L0_ffn_w1", "L0_ffn_w2", "L0_ffn_w3", "L0_ffn_sw1", "L0_ffn_sw2", "L0_ffn_sw3"]


def kernel(**inputs):
    import numpy as _np
    import concourse.bacc as _bacc
    from concourse import mybir as _mybir
    from concourse.bass_utils import run_bass_kernel_spmd as _run

    nc = _bacc.Bacc("TRN2", target_bir_lowering=False, num_devices=1)
    arrays, args = {}, []
    for name in _INS:
        a = _np.ascontiguousarray(inputs[name])
        arrays[f"in_{name}_dram"] = a
        args.append(nc.dram_tensor(f"in_{name}_dram", a.shape, _mybir.dt.from_np(a.dtype), kind="ExternalInput").ap())
    shape = inputs["x"].shape
    o = nc.dram_tensor("out_0_dram", tuple(shape), _mybir.dt.float32, kind="ExternalOutput").ap()
    xattn_ffn_kernel(nc, *args, o)
    r = _run(nc, [arrays], core_ids=[0])
    return r.results[0]["out_0_dram"]
```
